# Optimizing a Trainium2 kernel written in Bass

```python
import numpy as np
import jax
import jax.numpy as jnp

def _softmax(x, axis=-1):
    return jax.nn.softmax(x, axis=axis)

def _gelu(x):
    return jax.nn.gelu(x, approximate=True)

def _silu(x):
    return jax.nn.silu(x)

def _sigmoid(x):
    return jax.nn.sigmoid(x)

def _layernorm(x, axis=-1, eps=1e-05):
    m = jnp.mean(x, axis=axis, keepdims=True)
    v = jnp.var(x, axis=axis, keepdims=True)
    return (x - m) / jnp.sqrt(v + eps)

def _scatter_add(tgt, idx, src, axis=0):
    return tgt.at[idx].add(src)

def _segment_sum(src, seg, n):
    return jax.ops.segment_sum(src, seg, n)
kernel_name = 'mk_decoder_postln_d1_seqx_r8_c13286'

def setup_inputs(seed: int=0):
    np.random.seed(seed)
    _w = jnp.asarray

    def _rec_inputs():
        import jax
        import jax.numpy as jnp
        _rk = jax.random.key(seed)
        x = -0.0002928 + 1 * jax.random.normal(jax.random.fold_in(_rk, 1), (16, 128, 128), jnp.float32)
        _lenS = 128 - jax.random.randint(jax.random.fold_in(_rk, 7), (16,), 0, max(1, 128 // 4) + 1, jnp.int32)
        _lenS2 = 128 - jax.random.randint(jax.random.fold_in(_rk, 8), (16,), 0, max(1, 128 // 4) + 1, jnp.int32)
        _ctx_1024P = jax.random.normal(jax.random.fold_in(_rk, 11), (16, 16, 128), jnp.float32)
        _ctx_1024c = jax.random.dirichlet(jax.random.fold_in(_rk, 511), 0.3 * jnp.ones((16,), jnp.float32), (16, 128))
        _ctx_1024t = jnp.einsum('bsk,bkd->bsd', _ctx_1024c, _ctx_1024P)
        _ctx_1024t = _ctx_1024t * jax.lax.rsqrt(jnp.mean(jnp.square(_ctx_1024t)) + 1e-12) * 0.953939
        ctx_1024 = -0.000514642 + 1.00011 * (_ctx_1024t + 0.3 * jax.random.normal(jax.random.fold_in(_rk, 611), (16, 128, 128), jnp.float32))
        return (x, ctx_1024)
    x, ctx_1024 = _rec_inputs()

    def _L0_attn_setup():
        import jax, jax.numpy as jnp
        import numpy as np
        EPS_LN = 1e-06
        STAB = 0.001

        def layer_norm(x, gamma, beta):
            mu = jnp.mean(x, axis=-1, keepdims=True)
            var = jnp.mean(jnp.square(x - mu), axis=-1, keepdims=True)
            return (x - mu) * jax.lax.rsqrt(var + EPS_LN) * gamma + beta
        key = jax.random.key(seed)
        B, L, E, H, F = (8, 256, 128, 16, 512)
        dh = E // H
        ks = jax.random.split(key, 12)
        s_attn = 1.0 / np.sqrt(E)
        s_ffn1 = 1.0 / np.sqrt(E)
        s_ffn2 = 1.0 / np.sqrt(F)
        return {'x': jax.random.normal(ks[0], (B, L, E), jnp.float32), 'gamma1': jnp.ones((E,), jnp.float32), 'beta1': jnp.zeros((E,), jnp.float32), 'wq': jax.random.normal(ks[1], (E, H, dh), jnp.float32) * s_attn, 'wk': jax.random.normal(ks[2], (E, H, dh), jnp.float32) * s_attn, 'wv': jax.random.normal(ks[3], (E, H, dh), jnp.float32) * s_attn, 'wo': jax.random.normal(ks[4], (H, dh, E), jnp.float32) * s_attn, 'w1': jax.random.normal(ks[5], (E, F), jnp.float32) * s_ffn1, 'b1': jnp.zeros((F,), jnp.float32), 'w2': jax.random.normal(ks[6], (F, E), jnp.float32) * s_ffn2, 'b2': jnp.zeros((E,), jnp.float32)}
    _L0_attn_all = _L0_attn_setup()
    _L0_attn_in = {k: v for k, v in _L0_attn_all.items() if k in ('gamma1', 'beta1', 'wq', 'wk', 'wv', 'wo', 'w1', 'b1', 'w2', 'b2')}
    del _L0_attn_all

    def _L0_xattn_setup():
        import jax, jax.numpy as jnp
        import numpy as np
        EPS = 1e-06
        ROPE_THETA = 10000.0

        def _layernorm(x, w, b):
            mu = jnp.mean(x, axis=-1, keepdims=True)
            var = jnp.var(x, axis=-1, keepdims=True)
            return (x - mu) * jax.lax.rsqrt(var + EPS) * w + b

        def _apply_rope(q):
            b, h, s, d = q.shape
            inv_freq = 1.0 / ROPE_THETA ** (jnp.arange(0, d, 2, dtype=jnp.float32) / d)
            ang = jnp.arange(s, dtype=jnp.float32)[:, None] * inv_freq[None, :]
            cos = jnp.cos(ang)[None, None]
            sin = jnp.sin(ang)[None, None]
            qp = q.reshape(b, h, s, d // 2, 2)
            qe, qo = (qp[..., 0], qp[..., 1])
            out = jnp.stack([qe * cos - qo * sin, qe * sin + qo * cos], axis=-1)
            return out.reshape(b, h, s, d)
        key = jax.random.key(seed)
        ks = jax.random.split(key, 8)
        b, s1, s2, qdim, kdim, H = (2, 256, 128, 128, 128, 16)
        hd = qdim // H
        sc = 0.02
        return {'x': jax.random.normal(ks[0], (b, s1, qdim), jnp.float32), 'y': jax.random.normal(ks[1], (b, s2, kdim), jnp.float32), 'q_w': jax.random.normal(ks[2], (qdim, qdim), jnp.float32) * sc, 'q_b': jnp.zeros((qdim,), jnp.float32), 'kv_w': jax.random.normal(ks[3], (2 * qdim, kdim), jnp.float32) * sc, 'kv_b': jnp.zeros((2 * qdim,), jnp.float32), 'qn_w': jnp.ones((hd,), jnp.float32), 'qn_b': jnp.zeros((hd,), jnp.float32), 'kn_w': jnp.ones((hd,), jnp.float32), 'kn_b': jnp.zeros((hd,), jnp.float32), 'out_w': jax.random.normal(ks[4], (qdim, qdim), jnp.float32) * sc, 'out_b': jnp.zeros((qdim,), jnp.float32)}
    _L0_xattn_all = _L0_xattn_setup()
    _L0_xattn_in = {k: v for k, v in _L0_xattn_all.items() if k in ('q_w', 'q_b', 'kv_w', 'kv_b', 'qn_w', 'qn_b', 'kn_w', 'kn_b', 'out_w', 'out_b')}
    del _L0_xattn_all

    def _L0_ffn_setup():
        import jax, jax.numpy as jnp
        import numpy as np
        HIDDEN = 128
        NUM_EXPERTS = 8
        TOP_K = 2
        B, S = (2, 256)
        key = jax.random.key(seed)
        k1, k2, k3, k4, k5 = jax.random.split(key, 5)
        d, dff, E = (HIDDEN, 4 * HIDDEN, NUM_EXPERTS)
        x = jax.random.normal(k1, (B, S, d), dtype=jnp.float32)
        W1 = jax.random.normal(k2, (E, d, dff), dtype=jnp.float32) * (1.0 / np.sqrt(d))
        b1 = jax.random.normal(k3, (E, dff), dtype=jnp.float32) * 0.01
        W2 = jax.random.normal(k4, (E, dff, d), dtype=jnp.float32) * (1.0 / np.sqrt(dff))
        b2 = jax.random.normal(k5, (E, d), dtype=jnp.float32) * 0.01
        return {'x': x, 'W1': W1, 'b1': b1, 'W2': W2, 'b2': b2}
    _L0_ffn_all = _L0_ffn_setup()
    _L0_ffn_in = {k: v for k, v in _L0_ffn_all.items() if k in ('W1', 'b1', 'W2', 'b2')}
    del _L0_ffn_all
    return {'x': x, 'ctx_1024': ctx_1024, 'L0_attn_gamma1': _L0_attn_in['gamma1'], 'L0_attn_beta1': _L0_attn_in['beta1'], 'L0_attn_wq': _L0_attn_in['wq'], 'L0_attn_wk': _L0_attn_in['wk'], 'L0_attn_wv': _L0_attn_in['wv'], 'L0_attn_wo': _L0_attn_in['wo'], 'L0_attn_w1': _L0_attn_in['w1'], 'L0_attn_b1': _L0_attn_in['b1'], 'L0_attn_w2': _L0_attn_in['w2'], 'L0_attn_b2': _L0_attn_in['b2'], 'L0_xattn_q_w': _L0_xattn_in['q_w'], 'L0_xattn_q_b': _L0_xattn_in['q_b'], 'L0_xattn_kv_w': _L0_xattn_in['kv_w'], 'L0_xattn_kv_b': _L0_xattn_in['kv_b'], 'L0_xattn_qn_w': _L0_xattn_in['qn_w'], 'L0_xattn_qn_b': _L0_xattn_in['qn_b'], 'L0_xattn_kn_w': _L0_xattn_in['kn_w'], 'L0_xattn_kn_b': _L0_xattn_in['kn_b'], 'L0_xattn_out_w': _L0_xattn_in['out_w'], 'L0_xattn_out_b': _L0_xattn_in['out_b'], 'L0_ffn_W1': _L0_ffn_in['W1'], 'L0_ffn_b1': _L0_ffn_in['b1'], 'L0_ffn_W2': _L0_ffn_in['W2'], 'L0_ffn_b2': _L0_ffn_in['b2']}

def reference(x, ctx_1024, L0_attn_gamma1, L0_attn_beta1, L0_attn_wq, L0_attn_wk, L0_attn_wv, L0_attn_wo, L0_attn_w1, L0_attn_b1, L0_attn_w2, L0_attn_b2, L0_xattn_q_w, L0_xattn_q_b, L0_xattn_kv_w, L0_xattn_kv_b, L0_xattn_qn_w, L0_xattn_qn_b, L0_xattn_kn_w, L0_xattn_kn_b, L0_xattn_out_w, L0_xattn_out_b, L0_ffn_W1, L0_ffn_b1, L0_ffn_W2, L0_ffn_b2):
    import jax
    import jax.numpy as jnp

    def _L0_attn_ref(x, gamma1, beta1, wq, wk, wv, wo, w1, b1, w2, b2):
        import jax, jax.numpy as jnp
        import numpy as np
        EPS_LN = 1e-06
        STAB = 0.001

        def layer_norm(x, gamma, beta):
            mu = jnp.mean(x, axis=-1, keepdims=True)
            var = jnp.mean(jnp.square(x - mu), axis=-1, keepdims=True)
            return (x - mu) * jax.lax.rsqrt(var + EPS_LN) * gamma + beta
        ln1 = layer_norm(x, gamma1, beta1)
        q = jnp.einsum('ble,ehd->blhd', ln1, wq)
        k = jnp.einsum('ble,ehd->blhd', ln1, wk)
        v = jnp.einsum('ble,ehd->blhd', ln1, wv)
        qp = jax.nn.relu(q) + STAB
        kp = jax.nn.relu(k) + STAB
        kvs = jnp.einsum('blhm,blhd->bhmd', kp, v)
        num = jnp.einsum('blhm,bhmd->blhd', qp, kvs)
        ksum = jnp.sum(kp, axis=1)
        den = jnp.einsum('blhm,bhm->blh', qp, ksum)
        att = num / den[..., None]
        attn_out = jnp.einsum('blhd,hde->ble', att, wo)
        add1 = attn_out + x
        ln2 = layer_norm(add1, gamma1, beta1)
        h = jax.nn.gelu(jnp.einsum('ble,ef->blf', ln2, w1) + b1, approximate=False)
        out2 = jax.nn.gelu(jnp.einsum('blf,fe->ble', h, w2) + b2, approximate=False)
        return out2 + add1

    def _L0_xattn_ref(x, y, q_w, q_b, kv_w, kv_b, qn_w, qn_b, kn_w, kn_b, out_w, out_b):
        import jax, jax.numpy as jnp
        import numpy as np
        EPS = 1e-06
        ROPE_THETA = 10000.0

        def _layernorm(x, w, b):
            mu = jnp.mean(x, axis=-1, keepdims=True)
            var = jnp.var(x, axis=-1, keepdims=True)
            return (x - mu) * jax.lax.rsqrt(var + EPS) * w + b

        def _apply_rope(q):
            b, h, s, d = q.shape
            inv_freq = 1.0 / ROPE_THETA ** (jnp.arange(0, d, 2, dtype=jnp.float32) / d)
            ang = jnp.arange(s, dtype=jnp.float32)[:, None] * inv_freq[None, :]
            cos = jnp.cos(ang)[None, None]
            sin = jnp.sin(ang)[None, None]
            qp = q.reshape(b, h, s, d // 2, 2)
            qe, qo = (qp[..., 0], qp[..., 1])
            out = jnp.stack([qe * cos - qo * sin, qe * sin + qo * cos], axis=-1)
            return out.reshape(b, h, s, d)
        b, s1, c = x.shape
        _, s2, _ = y.shape
        H = 16
        hd = c // H
        scale = hd ** (-0.5)
        q = (x @ q_w.T + q_b).reshape(b, s1, H, hd).transpose(0, 2, 1, 3)
        kv = (y @ kv_w.T + kv_b).reshape(b, s2, 2, H, hd).transpose(2, 0, 3, 1, 4)
        k, v = (kv[0], kv[1])
        q = _layernorm(q, qn_w, qn_b)
        k = _layernorm(k, kn_w, kn_b)
        q = _apply_rope(q) * scale
        attn = jnp.einsum('bhqd,bhkd->bhqk', q, k)
        attn = jax.nn.softmax(attn, axis=-1)
        o = jnp.einsum('bhqk,bhkd->bhqd', attn, v)
        o = o.transpose(0, 2, 1, 3).reshape(b, s1, c)
        return o @ out_w.T + out_b

    def _L0_ffn_ref(x, W1, b1, W2, b2):
        import jax, jax.numpy as jnp
        import numpy as np
        HIDDEN = 128
        NUM_EXPERTS = 8
        TOP_K = 2
        B, S = (2, 256)
        Bm, Sm, d = x.shape
        E = W1.shape[0]
        x_flat = x.reshape(-1, d)
        h = jnp.mod(x_flat[:, :TOP_K].sum(axis=1).astype(jnp.int32), E)
        sel = jnp.stack([h, jnp.mod(h + 1, E)], axis=1)

        def step(acc, params):
            e, W1e, b1e, W2e, b2e = params
            w = jnp.any(sel == e, axis=1).astype(x.dtype) / TOP_K
            y = jnp.maximum(x_flat @ W1e + b1e, 0.0) @ W2e + b2e
            return (acc + w[:, None] * y, None)
        init = jnp.zeros_like(x_flat)
        out_flat, _ = jax.lax.scan(step, init, (jnp.arange(E), W1, b1, W2, b2))
        return out_flat.reshape(Bm, Sm, d)
    x = _layernorm(x + _L0_attn_ref(x, L0_attn_gamma1, L0_attn_beta1, L0_attn_wq, L0_attn_wk, L0_attn_wv, L0_attn_wo, L0_attn_w1, L0_attn_b1, L0_attn_w2, L0_attn_b2), axis=-1)
    x = _layernorm(x + _L0_xattn_ref(x, ctx_1024, L0_xattn_q_w, L0_xattn_q_b, L0_xattn_kv_w, L0_xattn_kv_b, L0_xattn_qn_w, L0_xattn_qn_b, L0_xattn_kn_w, L0_xattn_kn_b, L0_xattn_out_w, L0_xattn_out_b), axis=-1)
    x = _layernorm(x + _L0_ffn_ref(x, L0_ffn_W1, L0_ffn_b1, L0_ffn_W2, L0_ffn_b2), axis=-1)
    return x

_drawn_inputs = setup_inputs


def setup_inputs(seed=0):
    import zlib

    import numpy as np

    out = dict(_drawn_inputs(seed))
    spreads = {'L0_attn_gamma1': (1.0, 0.2),
     'L0_attn_beta1': (0.0, 0.1),
     'L0_attn_b1': (0.0, 0.1),
     'L0_attn_b2': (0.0, 0.1),
     'L0_xattn_q_b': (0.0, 0.529),
     'L0_xattn_kv_b': (0.0, 0.1),
     'L0_xattn_qn_w': (1.0, 0.6),
     'L0_xattn_qn_b': (0.0, 1.527),
     'L0_xattn_kn_w': (1.0, 0.6),
     'L0_xattn_kn_b': (0.0, 2.0),
     'L0_xattn_out_b': (0.0, 0.1)}
    factors = {'L0_ffn_b1': 8.0, 'L0_ffn_b2': 8.0}
    for name, (base, spread) in spreads.items():
        noise = np.random.default_rng([zlib.crc32(name.encode()), seed]).standard_normal(out[name].shape)
        drawn = base * np.exp(spread * noise) if base else spread * noise
        out[name] = jnp.asarray(drawn.astype(out[name].dtype))
    for name, factor in factors.items():
        out[name] = (out[name] * factor).astype(out[name].dtype)
    return out
```

```python
from contextlib import ExitStack

import numpy as np

import concourse.bass as bass
from concourse import mybir

F32 = mybir.dt.float32
BF16 = mybir.dt.bfloat16
I32 = mybir.dt.int32
U32 = mybir.dt.uint32
ALU = mybir.AluOpType
ACT = mybir.ActivationFunctionType
AX = mybir.AxisListType

P = 128
B = 16
H = 16
HD = 8
GB = 4
G = B // GB
W = GB * P
NTOK = B * P
NF = 4
NE = 8
SLOTS = B + NE - 1
ROW = P + 4
STAB = 0.001
NO_TOKEN = 65536.0
TERMS_K = (0, 0, 0, 1, 1, 2)
TERMS_Q = (0, 1, 2, 0, 1, 0)
KROWS = HD * len(TERMS_K)
HALF = 64

CONSTS = ("ident", "center", "mean8", "same_head", "rotate", "cos", "sin", "lower", "ones", "row0")


def constants():
    i = np.arange(P)
    same = (i[:, None] // HD == i[None, :] // HD).astype(np.float32)
    freq = 1.0 / 10000.0 ** (np.arange(0, HD, 2, dtype=np.float32) / HD)
    ang = np.arange(P, dtype=np.float32)[None, :] * freq[(i % HD) // 2][:, None]
    scale = HD ** -0.5
    rot = np.zeros((P, P), np.float32)
    rot[i[1::2], i[0::2]] = -1.0
    rot[i[0::2], i[1::2]] = 1.0
    row0 = np.zeros((P, P), np.float32)
    row0[0] = 1.0
    mats = {
        "ident": np.eye(P), "center": np.eye(P) - same / HD, "mean8": same / HD, "same_head": same,
        "rotate": rot, "cos": np.cos(ang) * scale, "sin": np.sin(ang) * scale,
        "lower": (i[:, None] < i[None, :]), "ones": np.ones((P, P)), "row0": row0,
    }
    small = np.zeros((P, 64), np.float32)
    small[:, 0:H] = i[:, None] // HD == np.arange(H)[None, :]
    small[:, 16:16 + NE] = np.arange(NE)[None, :]
    small[:, 32:48] = i[:, None] + P * np.arange(B)[None, :]
    return np.ascontiguousarray(np.concatenate([mats[n].astype(np.float32) for n in CONSTS] + [small], 1))


def decoder_layer(nc, x, ctx_in, gamma1, beta1, wq, wk, wv, wo, w1, b1, w2, b2, q_w, q_b, kv_w, kv_b,
                  qn_w, qn_b, kn_w, kn_b, out_w, out_b, eW1, eb1, eW2, eb2, consts, ones_row, out):
    q_scr = nc.dram_tensor("q_parts_scratch", (3, P, NTOK), BF16).ap()
    k_scr = nc.dram_tensor("k_parts_scratch", (3, P, NTOK), BF16).ap()
    sorted_scr = nc.dram_tensor("sorted_scratch", (SLOTS * P, ROW), F32).ap()
    out_rows = out.rearrange("b s e -> (b s) e")

    with ExitStack() as ctx:
        def sb(name, shape, dt=F32):
            return ctx.enter_context(nc.sbuf_tensor(name, shape, dt))

        def sem(name):
            return ctx.enter_context(nc.semaphore(name))

        X = sb("X", [P, NTOK])
        N = sb("N", [P, NTOK])
        LNT = sb("LNT", [P, NTOK])
        QP = sb("QP", [P, NTOK])
        KP = sb("KP", [P, NTOK])
        V = sb("V", [P, NTOK])
        ADD = sb("ADD", [P, NTOK])
        CTX = sb("CTX", [P, NTOK])
        KVS = sb("KVS", [P, B, P + H + 4])
        PART = sb("PART", [P, 2, 3, W], BF16)
        QPK = sb("QPK", [P, H // 2, NTOK], BF16)
        KPK = sb("KPK", [P, H // 2, NTOK], BF16)
        EW1 = sb("EW1", [P, NE, NF * P])
        EW2 = sb("EW2", [P, NE, NF, P])
        VAUG = sb("VAUG", [P, B, H, HD + 1])
        EXPS = CTX[:, :].rearrange("p (r w) -> p r w", r=4)
        qpk_f = QPK[:, :, :].rearrange("p i t -> p (i t)").bitcast(F32)
        kpk_f = KPK[:, :, :].rearrange("p i t -> p (i t)").bitcast(F32)
        HT = qpk_f[:, 0:4096].rearrange("p (r c w) -> p r c w", r=2, c=NF)
        CTXT = qpk_f[:, 4096:6144]
        X2 = KVS[:, :, 0:ROW]
        XS = kpk_f[:, 0:SLOTS * ROW].rearrange("p (s r) -> p s r", s=SLOTS)
        XST = qpk_f[:, 0:SLOTS * P]
        HE = kpk_f[:, SLOTS * ROW:SLOTS * ROW + 2 * NF * P].rearrange("p (c t) -> p c t", c=2 * NF)

        C = sb("C", [P, len(CONSTS) * P + 64])
        K = {n: C[:, i * P:(i + 1) * P] for i, n in enumerate(CONSTS)}
        head_mask = C[:, len(CONSTS) * P:len(CONSTS) * P + H]
        expert_no = C[:, len(CONSTS) * P + 16:len(CONSTS) * P + 16 + NE]
        token_no = C[:, len(CONSTS) * P + 32:len(CONSTS) * P + 48]
        WQ = sb("WQ", [P, P])
        WKV = sb("WKV", [P, 2 * P])
        WO = sb("WO", [P, P])
        W1 = sb("W1", [P, NF * P])
        W2 = sb("W2", [P, NF, P])
        XW = sb("XW", [P, 4, P])
        XWT = sb("XWT", [P, 4, P])
        cols = sb("cols", [P, 24])
        GAMMA, BETA, QB, KB, QNW, QNB, KNW, KNB, QBC, KBC = (cols[:, i:i + 1] for i in range(10))
        B1C = cols[:, 12:16]
        rows = sb("rows", [P, 3, P])
        EB1 = sb("EB1", [P, NE, NF])
        EB2 = LNT[:, NE * P:2 * NE * P].rearrange("p (e d) -> p e d", e=NE)
        EB2P = LNT[:, 0:NE * P].rearrange("p (e d) -> p e d", e=NE)
        st = sb("st", [P, B, 6])
        mv = sb("mv", [P, 4, B, 2])
        lnv = sb("lnv", [P, 4, B])
        rstd = sb("rstd", [P, 4, B])
        RD = sb("RD", [P, B, H])
        M = sb("M", [P, 2, H])
        NEGM = sb("NEGM", [H, 2, P], BF16)
        rt = sb("rt", [P, 8, B])
        rti = sb("rti", [P, 2, B], I32)
        posu = sb("posu", [P, B], U32)
        OH = V[:, 0:P].rearrange("p (b e) -> p b e", e=NE)
        tot = V[:, P:3 * P].rearrange("p (a b e) -> p a b e", a=2, e=NE)
        rank = V[:, 3 * P:4 * P].rearrange("p (b e) -> p b e", e=NE)
        cnt = sb("cnt", [P, 4, NE])
        cnti = sb("cnti", [P, 2, NE + 1], I32)
        starts = sb("starts", [P, 2, NE + 1])
        fill = sb("fill", [P, ROW])
        XBS = ADD[:, 0:P]
        RES = ADD[:, P:3 * P].rearrange("p (a e) -> p a e", a=2)
        OUTN = ADD[:, 3 * P:4 * P]
        est = sb("est", [P, 6])
        emv = sb("emv", [P, 4])
        tok_f = sb("tok_f", [P, 2])
        tok_u = sb("tok_u", [P, 1], U32)
        ps = ctx.enter_context(nc.psum_tensor("ps", [P, 8, W], F32))

        def cs(g):
            return slice(g * W, (g + 1) * W)

        def blk(t, b):
            return t[:, b * P:(b + 1) * P]

        def rows_of(t, g):
            return t[:, cs(g)].rearrange("p (b e) -> p b e", b=GB)

        def bank_rows(bank):
            return ps[:, bank, :].rearrange("p (b e) -> p b e", b=GB)

        ld_x = [sem(f"ld_x{g}") for g in range(G)]
        ld_const = sem("ld_const")
        ld_attn = sem("ld_attn")
        ld_ctx = sem("ld_ctx")
        ld_xw = sem("ld_xw")
        ld_small = sem("ld_small")
        ld_exp = sem("ld_exp")
        ld_eb2 = sem("ld_eb2")
        ld_ones = sem("ld_ones")
        s_mv = [sem(f"s_mv{n}") for n in range(3)]
        s_lnv = [sem(f"s_lnv{n}") for n in range(3)]
        s_rstd = [sem(f"s_rstd{n}") for n in range(3)]
        s_st = sem("s_st")
        s_norm = [sem(f"s_norm{n}") for n in range(3)]
        s_nT = [sem(f"s_nT{n}") for n in range(3)]
        s_lnT = [sem(f"s_lnT{n}") for n in range(3)]
        s_q = sem("s_q"); s_kv = sem("s_kv")
        s_qp = sem("s_qp"); s_kp = sem("s_kp"); s_v = sem("s_v")
        s_kvs = sem("s_kvs"); s_kvsm = sem("s_kvsm")
        s_num = sem("s_num"); s_rd1 = sem("s_rd1"); s_att = sem("s_att")
        s_attT = sem("s_attT"); s_attTs = sem("s_attTs")
        s_ao = sem("s_ao"); s_add = sem("s_add"); s_2x = sem("s_2x")
        s_f1 = sem("s_f1"); s_g1 = sem("s_g1")
        s_f2 = sem("s_f2"); s_g2 = sem("s_g2"); s_y = sem("s_y")
        s_x1b = sem("s_x1b")
        s_prep = sem("s_prep"); s_xwt = sem("s_xwt")
        s_cT = sem("s_cT"); s_cTs = sem("s_cTs")
        s_kc = sem("s_kc"); s_v2 = sem("s_v2"); s_va1 = sem("s_va1"); s_vaug = sem("s_vaug")
        s_sq = [sem("s_sq_k"), sem("s_sq_q")]
        s_var = [sem("s_var_k"), sem("s_var_q")]
        s_lv = [sem("s_lv_k"), sem("s_lv_q")]
        s_rs = [sem("s_rs_k"), sem("s_rs_q")]
        s_n8 = [sem("s_n8_k"), sem("s_n8_q")]
        s_aff = [sem("s_aff_k"), sem("s_aff_q")]
        s_hi = [sem("s_hi_k"), sem("s_hi_q")]
        s_r1 = [sem("s_r1_k"), sem("s_r1_q")]
        s_mid = [sem("s_mid_k"), sem("s_mid_q")]
        s_lo = [sem("s_lo_k"), sem("s_lo_q")]
        s_scr = [sem("s_scr_k"), sem("s_scr_q")]
        s_pack = [[sem(f"s_pack_k{g}") for g in range(G)], [sem(f"s_pack_q{g}") for g in range(G)]]
        s_qc = sem("s_qc"); s_rot = sem("s_rot"); s_t1 = sem("s_t1"); s_t2 = sem("s_t2"); s_qh = sem("s_qh")
        s_sm = sem("s_sm"); s_max = sem("s_max")
        s_mT = sem("s_mT"); s_negm = sem("s_negm")
        s_mrow = [sem("s_mrow0"), sem("s_mrow1")]
        s_sc = sem("s_sc"); s_exp = sem("s_exp"); s_pv = sem("s_pv")
        s_rd2 = sem("s_rd2"); s_on = sem("s_on")
        s_oT = sem("s_oT"); s_oTs = sem("s_oTs"); s_pr = sem("s_pr"); s_y2 = sem("s_y2"); s_x2 = sem("s_x2")
        s_x2id = sem("s_x2id")
        s_rt = sem("s_rt")
        s_oh = sem("s_oh"); s_rank = sem("s_rank")
        s_pos = sem("s_pos"); s_cnt = sem("s_cnt")
        s_fillm = sem("s_fillm"); s_sort = sem("s_sort"); s_xs = sem("s_xs")
        s_xsT = sem("s_xsT"); s_xst = sem("s_xst")
        s_eb2 = sem("s_eb2")
        s_h = sem("s_h"); s_ha = sem("s_ha"); s_hb = sem("s_hb"); s_ye = sem("s_ye")
        s_xb = sem("s_xb"); s_res = sem("s_res"); s_est = sem("s_est"); s_emv = sem("s_emv")
        s_elv = sem("s_elv"); s_ers = sem("s_ers"); s_outn = sem("s_outn")
        s_tokf = sem("s_tokf"); s_tok = sem("s_tok"); s_out = sem("s_out")

        block = ctx.enter_context(nc.Block())

        @block.sync
        def _(sp):
            xv = x.rearrange("b s e -> s b e")
            for g in range(G):
                sp.dma_start(rows_of(X, g), xv[:, g * GB:(g + 1) * GB, :]).then_inc(ld_x[g], 16)
            sp.dma_start(C[:, :], consts).then_inc(ld_const, 16)
            col = lambda v: v.rearrange("(p a) -> p a", a=1)
            sp.dma_start(GAMMA, col(gamma1)).then_inc(ld_small, 16)
            sp.dma_start(BETA, col(beta1)).then_inc(ld_small, 16)
            sp.dma_start(WQ[:, :], wq.rearrange("e h d -> e (h d)")).then_inc(ld_attn, 16)
            sp.dma_start(WKV[:, 0:P], wk.rearrange("e h d -> e (h d)")).then_inc(ld_attn, 16)
            sp.dma_start(WKV[:, P:2 * P], wv.rearrange("e h d -> e (h d)")).then_inc(ld_attn, 16)
            sp.dma_start(WO[:, :], wo.rearrange("h d e -> (h d) e")).then_inc(ld_attn, 16)
            sp.dma_start(W1[:, :], w1).then_inc(ld_attn, 16)
            sp.dma_start(W2[:, :, :], w2.rearrange("(c p) e -> p c e", p=P)).then_inc(ld_attn, 16)
            sp.dma_start(B1C, b1).then_inc(ld_small, 16)
            sp.dma_start(rows[:, 0, :], b2.partition_broadcast(P)).then_inc(ld_small, 16)
            sp.dma_start(QB, col(q_b)).then_inc(ld_small, 16)
            sp.dma_start(KB, col(kv_b[0:P])).then_inc(ld_small, 16)
            sp.dma_start(rows[:, 1, :], kv_b[P:2 * P].partition_broadcast(P)).then_inc(ld_small, 16)
            sp.dma_start(rows[:, 2, :], out_b.partition_broadcast(P)).then_inc(ld_small, 16)
            for dst, src in ((QNW, qn_w), (QNB, qn_b), (KNW, kn_w), (KNB, kn_b)):
                sp.dma_start(dst, src).then_inc(ld_small, 16)
            sp.dma_start(XW[:, 0, :], q_w).then_inc(ld_xw, 16)
            sp.dma_start(XW[:, 1:3, :], kv_w.rearrange("(t p) i -> p t i", p=P)).then_inc(ld_xw, 16)
            sp.dma_start(XW[:, 3, :], out_w).then_inc(ld_xw, 16)
            sp.dma_start(CTX[:, :].rearrange("p (b e) -> p b e", b=B), ctx_in.rearrange("b s e -> s b e")).then_inc(ld_ctx, 16)
            sp.dma_start(EB1[:, :, :], eb1).then_inc(ld_exp, 16)
            sp.dma_start(EW1[:, :, :], eW1.rearrange("e d f -> d e f")).then_inc(ld_exp, 16)
            sp.dma_start(EW2[:, :, :, :], eW2.rearrange("e (c p) d -> p e c d", p=P)).then_inc(ld_exp, 16)
            for r in (KROWS, HALF + KROWS):
                sp.dma_start(KPK[r:r + 1, :, :], ones_row).then_inc(ld_ones, 16)
            for t, (scr, pack, terms) in enumerate(((k_scr, KPK, TERMS_K), (q_scr, QPK, TERMS_Q))):
                for g in range(G):
                    sp.wait_ge(s_lo[t], g + 1)
                    sp.wait_ge(s_mid[t], g + 1)
                    sp.dma_start(scr.rearrange("t p s -> p t s")[:, :, cs(g)],
                                 PART[:, g % 2, :, :]).then_inc(s_scr[t], 16)
                    sp.wait_ge(s_scr[t], 16 * (g + 1))
                    if t == 1 and g == 0:
                        sp.wait_ge(s_kc, G)
                        sp.wait_ge(s_v2, G)
                        sp.wait_ge(s_f2, G)
                    for par in range(2):
                        src = scr.rearrange("t (i r d) s -> t r d i s", r=2, d=HD)
                        for n, part in enumerate(terms):
                            sp.dma_start(pack[HALF * par + HD * n:HALF * par + HD * (n + 1), :, cs(g)],
                                         src[part, par, :, :, cs(g)]).then_inc(s_pack[t][g], 16)
            sp.wait_ge(s_qc, G)
            for e in range(NE):
                sp.dma_start(EB2[:, e, :], eb2[e].partition_broadcast(P)).then_inc(ld_eb2, 16)
            for b in range(B):
                sp.wait_ge(s_negm, b + 1)
                for par in range(2):
                    r = HALF * par + KROWS
                    sp.dma_start(QPK[r:r + 1, :, b * P:(b + 1) * P],
                                 NEGM[par * 8:par * 8 + 8, b % 2, :]).then_inc(s_mrow[b % 2], 16)
            sp.wait_ge(s_sort, 16 * B)
            sp.wait_ge(s_sc, 4 * B)
            sp.dma_start(XS, sorted_scr.rearrange("(s p) r -> p s r", p=P)).then_inc(s_xs, 16)

        @block.tensor
        def _(pe):
            mm = nc.tensor.matmul

            def transposes(bank, src, g, done, k=GB):
                for j in range(k):
                    last = nc.tensor.transpose(ps[:, bank, j * P:(j + 1) * P], blk(src, g * GB + j), K["ident"])
                last.then_inc(done, 1)

            pe.wait_ge(ld_const, 16)
            pe.wait_ge(ld_xw, 48)
            pe.wait_ge(ld_small, 16 * 12)
            for n, right in enumerate((K["center"], K["center"], K["ident"], K["ident"])):
                mm(ps[:, 7, n * P:(n + 1) * P], XW[:, n, :], right, start=True, stop=True)
            mm(ps[:, 6, 0:1], K["center"], QB, start=True, stop=True)
            mm(ps[:, 6, 1:2], K["center"], KB, start=True, stop=True).then_inc(s_prep, 1)

            def norm_T(n):
                for g in range(G):
                    pe.wait_ge(s_norm[n], g + 1)
                    if g >= 2:
                        pe.wait_ge(s_lnT[n], g - 1)
                    transposes(g % 2, N, g, s_nT[n])

            norm_T(0)
            pe.wait_ge(ld_attn, 16 * 6)
            pe.wait_ge(s_xwt, 2)
            for g in range(G):
                pe.wait_ge(s_lnT[0], g + 1)
                if g >= 2:
                    pe.wait_ge(s_qp, g - 1)
                mm(ps[:, 2 + g % 2, :], WQ[:, :], LNT[:, cs(g)], start=True, stop=True).then_inc(s_q, 1)
                if g >= 2:
                    pe.wait_ge(s_kp, g - 1)
                    pe.wait_ge(s_v, g - 1)
                for i in range(2):
                    for j in range(GB):
                        last = mm(ps[:, 4 + 2 * (g % 2) + i, j * P:(j + 1) * P],
                                  blk(LNT, g * GB + j), WKV[:, i * P:(i + 1) * P], start=True, stop=True)
                    last.then_inc(s_kv, 1)
            for g in range(G):
                pe.wait_ge(s_kp, g + 1)
                pe.wait_ge(s_v, g + 1)
                if g == 0:
                    pe.wait_ge(s_lnT[0], G)
                    pe.wait_ge(s_qp, G)
                if g >= 2:
                    pe.wait_ge(s_kvsm, g - 1)
                for j in range(GB):
                    b = g * GB + j
                    mm(ps[:, g % 2, j * P:(j + 1) * P], blk(KP, b), blk(V, b), start=True, stop=True)
                    last = mm(ps[:, 2 + g % 2, j:j + 1], blk(KP, b), K["ones"][:, 0:1], start=True, stop=True)
                last.then_inc(s_kvs, 1)
            for g in range(G):
                pe.wait_ge(s_kvsm, g + 1)
                if g == 0:
                    pe.wait_ge(s_kp, G)
                    pe.wait_ge(s_v, G)
                if g >= 2:
                    pe.wait_ge(s_att, g - 1)
                for j in range(GB):
                    b = g * GB + j
                    last = mm(ps[:, 4 + 2 * (g % 2) + j // 2, (j % 2) * 2 * P:(j % 2) * 2 * P + P + H],
                              blk(QP, b), KVS[:, b, 0:P + H], start=True, stop=True)
                last.then_inc(s_num, 1)
            for g in range(G):
                pe.wait_ge(s_att, g + 1)
                if g == 0:
                    pe.wait_ge(s_kvsm, G)
                if g >= 2:
                    pe.wait_ge(s_attTs, g - 1)
                transposes(g % 2, KP, g, s_attT)
            for g in range(G):
                pe.wait_ge(s_attTs, g + 1)
                if g >= 2:
                    pe.wait_ge(s_add, g - 1)
                for j in range(GB):
                    last = mm(ps[:, 2 + g % 2, j * P:(j + 1) * P], blk(QP, g * GB + j), WO[:, :], start=True, stop=True)
                last.then_inc(s_ao, 1)
            pe.wait_ge(s_attTs, G)
            norm_T(1)

            def ffn1(g):
                pe.wait_ge(s_lnT[1], g + 1)
                for c in range(NF):
                    if g >= 1:
                        pe.wait_ge(s_g1, NF * (g - 1) + c + 1)
                    mm(ps[:, 4 + c, :], W1[:, c * P:(c + 1) * P], LNT[:, cs(g)], start=True, stop=True).then_inc(s_f1, 1)

            def ffn2(g):
                pe.wait_ge(s_g1, NF * (g + 1))
                if g == 0:
                    pe.wait_ge(s_add, G)
                if g >= 2:
                    pe.wait_ge(s_g2, g - 1)
                for j in range(GB):
                    o = ps[:, 2 + g % 2, j * P:(j + 1) * P]
                    for c in range(NF):
                        mm(o, HT[:, g % 2, c, j * P:(j + 1) * P], W2[:, c, :], start=(c == 0), stop=False)
                    last = mm(o, K["row0"], rows[:, 0, :], start=False, stop=True)
                last.then_inc(s_f2, 1)

            pe.wait_ge(s_att, G)
            for g in range(G + 1):
                if g < G:
                    ffn1(g)
                if g >= 1:
                    ffn2(g - 1)
            pe.wait_ge(ld_ctx, 16)
            pe.wait_ge(s_lnT[1], G)
            for g in range(G):
                if g >= 2:
                    pe.wait_ge(s_cTs, g - 1)
                transposes(g % 2, CTX, g, s_cT)
            for g in range(G):
                pe.wait_ge(s_cTs, g + 1)
                if g == 0:
                    pe.wait_ge(s_g2, G)
                if g >= 2:
                    pe.wait_ge(s_n8[0], g - 1)
                    pe.wait_ge(s_sq[0], g - 1)
                mm(ps[:, 2 + g % 2, :], XWT[:, 1, :], CTXT[:, cs(g)], start=True, stop=True).then_inc(s_kc, 1)
                if g == 0:
                    pe.wait_ge(s_g1, NF * G)
                if g >= 2:
                    pe.wait_ge(s_vaug, g - 1)
                for j in range(GB):
                    last = mm(ps[:, 4 + g % 2, j * P:(j + 1) * P], blk(CTXT, g * GB + j), XWT[:, 2, :], start=True, stop=True)
                last.then_inc(s_v2, 1)
                pe.wait_ge(s_sq[0], g + 1)
                if g >= 2:
                    pe.wait_ge(s_lv[0], g - 1)
                mm(ps[:, 6 + g % 2, :], K["mean8"], QP[:, cs(g)], start=True, stop=True).then_inc(s_var[0], 1)
            pe.wait_ge(s_cTs, G)
            norm_T(2)
            for g in range(G):
                pe.wait_ge(s_lnT[2], g + 1)
                if g == 0:
                    pe.wait_ge(s_n8[0], G)
                if g >= 2:
                    pe.wait_ge(s_n8[1], g - 1)
                mm(ps[:, 2 + g % 2, :], XWT[:, 0, :], LNT[:, cs(g)], start=True, stop=True).then_inc(s_qc, 1)
                pe.wait_ge(s_sq[1], g + 1)
                if g == 0:
                    pe.wait_ge(s_lv[0], G)
                if g >= 2:
                    pe.wait_ge(s_lv[1], g - 1)
                mm(ps[:, 6 + g % 2, :], K["mean8"], QP[:, cs(g)], start=True, stop=True).then_inc(s_var[1], 1)
            for g in range(G):
                pe.wait_ge(s_aff[1], g + 1)
                if g == 0:
                    pe.wait_ge(s_vaug, G)
                if g >= 2:
                    pe.wait_ge(s_t2, g - 1)
                mm(ps[:, 4 + g % 2, :], K["rotate"], V[:, cs(g)], start=True, stop=True).then_inc(s_rot, 1)

            def unit(u):
                b, r = divmod(u, 4)
                return b, r % 2, r // 2

            def scores_for_max(u):
                b, par, half = unit(u)
                if u % (4 * GB) == 0:
                    pe.wait_ge(s_pack[0][b // GB], 16 * 12)
                    pe.wait_ge(s_pack[1][b // GB], 16 * 12)
                if u == 0:
                    pe.wait_ge(s_lnT[2], G)
                if u >= 2:
                    pe.wait_ge(s_max, u - 1)
                t = slice(b * P, (b + 1) * P)
                for j in range(4):
                    last = mm(ps[:, u % 2, j * P:(j + 1) * P], QPK[HALF * par:HALF * par + KROWS, 4 * half + j, t],
                              KPK[HALF * par:HALF * par + KROWS, 4 * half + j, t], start=True, stop=True)
                last.then_inc(s_sm, 1)

            def max_T(b):
                pe.wait_ge(s_max, 4 * (b + 1))
                if b == 0:
                    pe.wait_ge(s_lv[1], G)
                if b >= 1:
                    pe.wait_ge(s_negm, b)
                nc.tensor.transpose(ps[0:H, 7, 0:P], M[:, b % 2, :], K["ident"]).then_inc(s_mT, 1)

            def scores(u):
                b, par, half = unit(u)
                if u % 4 == 0:
                    pe.wait_ge(s_mrow[b % 2], 32 * (b // 2 + 1))
                if u == 0:
                    pe.wait_ge(ld_ones, 32)
                    pe.wait_ge(s_n8[1], G)
                    pe.wait_ge(s_t2, G)
                if u >= 3:
                    pe.wait_ge(s_exp, u - 2)
                t = slice(b * P, (b + 1) * P)
                for j in range(4):
                    last = mm(ps[:, 2 + u % 3, j * P:(j + 1) * P], KPK[HALF * par:HALF * par + KROWS + 1, 4 * half + j, t],
                              QPK[HALF * par:HALF * par + KROWS + 1, 4 * half + j, t], start=True, stop=True)
                last.then_inc(s_sc, 1)

            def times_v(u):
                b, par, half = unit(u)
                pe.wait_ge(s_exp, u + 1)
                if u % 4 == 0 and b >= 2:
                    pe.wait_ge(s_on, b - 1)
                if u == 0:
                    pe.wait_ge(s_vaug, G)
                for j in range(4):
                    h = 2 * (4 * half + j) + par
                    last = mm(ps[:, 5 + b % 2, h * 9:h * 9 + 9], EXPS[:, u % 4, j * P:(j + 1) * P], VAUG[:, b, h, :],
                              start=True, stop=True)
                last.then_inc(s_pv, 1)

            AHEAD = 2
            for b in range(AHEAD):
                for r in range(4):
                    scores_for_max(4 * b + r)
                max_T(b)
            for u in range(4 * B):
                b, r = divmod(u, 4)
                scores(u)
                if b + AHEAD < B:
                    scores_for_max(u + 4 * AHEAD)
                if u >= 2:
                    times_v(u - 2)
                if r == 0 and 1 <= b and b + AHEAD - 1 < B and b >= 1:
                    max_T(b + AHEAD - 1)
            times_v(4 * B - 2)
            times_v(4 * B - 1)
            for g in range(G):
                pe.wait_ge(s_on, GB * (g + 1))
                if g == 0:
                    pe.wait_ge(s_max, 4 * B)
                    pe.wait_ge(s_exp, 4 * B)
                if g >= 2:
                    pe.wait_ge(s_oTs, g - 1)
                transposes(g % 2, KP, g, s_oT)
            for g in range(G):
                pe.wait_ge(s_oTs, g + 1)
                if g >= 2:
                    pe.wait_ge(s_y2, g - 1)
                for j in range(GB):
                    last = mm(ps[:, 2 + g % 2, j * P:(j + 1) * P], blk(QP, g * GB + j), XWT[:, 3, :], start=True, stop=True)
                last.then_inc(s_pr, 1)
            pe.wait_ge(s_oh, 1)
            pe.wait_ge(s_negm, B)
            oh = OH[:, :, :].rearrange("p b e -> p (b e)")
            mm(ps[:, 7, 0:P], K["lower"], oh, start=True, stop=True)
            mm(ps[:, 7, P:2 * P], K["ones"], oh, start=True, stop=True).then_inc(s_rank, 1)
            pe.wait_ge(s_xs, 16)
            pe.wait_ge(s_oTs, G)
            for n in range((SLOTS + 3) // 4):
                if n >= 2:
                    pe.wait_ge(s_xst, n - 1)
                k = min(4, SLOTS - 4 * n)
                for j in range(k):
                    last = nc.tensor.transpose(ps[:, n % 2, j * P:(j + 1) * P], XS[:, 4 * n + j, 0:P], K["ident"])
                last.then_inc(s_xsT, 1)
            pe.wait_ge(s_xst, (SLOTS + 3) // 4)
            pe.wait_ge(s_y2, G)
            pe.sem_inc(s_ye, 1)
            pe.wait_ge(ld_exp, 16 * 3)
            reg = [pe.value_load(cnti[0:1, 1, h:h + 1], min_val=0, max_val=SLOTS) for h in range(NE + 1)]
            for h in range(NE):
                with pe.Fori(reg[h], reg[h + 1]) as t:
                    pe.wait_ge(s_hb, t + 1)
                    pe.wait_ge(s_ha, t + 1)
                    for c in range(2 * NF):
                        e = (h + c // NF) % NE
                        last = mm(ps[:, c // NF, (c % NF) * P:(c % NF + 1) * P], EW1[:, e, (c % NF) * P:(c % NF + 1) * P],
                                  XST[:, bass.ds(t * P, P)], start=True, stop=True)
                    last.then_inc(s_h, 1)
                    pe.wait_ge(s_ha, t + 2)
                    pe.wait_ge(s_hb, t + 2)
                    pe.wait_ge(s_res, t + 1)
                    for c in range(2 * NF):
                        e = (h + c // NF) % NE
                        last = mm(ps[:, 2, 0:P], HE[:, c, :], EW2[:, e, c % NF, :], start=(c == 0), stop=(c == 2 * NF - 1))
                    last.then_inc(s_ye, 1)

        @block.scalar
        def _(act):
            A = nc.scalar.activation

            def inv_std(n, g, eps):
                act.wait_ge(s_mv[n], g + 1)
                b = slice(g * GB, (g + 1) * GB)
                A(lnv[:, n, b], mv[:, n, b, 1], ACT.Ln, bias=eps).then_inc(s_lnv[n], 1)
                act.wait_ge(s_lnv[n], g + 1)
                A(rstd[:, n, b], lnv[:, n, b], ACT.Exp, scale=-0.5).then_inc(s_rstd[n], 1)

            nc.scalar.preload_act_table_set("natural_log_exp_and_others")
            for g in range(G):
                inv_std(0, g, 1e-6)
            act.wait_ge(s_prep, 1)
            nc.scalar.copy(XWT[:, :, :].rearrange("p n e -> p (n e)"), ps[:, 7, :]).then_inc(s_xwt, 1)
            nc.scalar.copy(cols[:, 8:10], ps[:, 6, 0:2]).then_inc(s_xwt, 1)

            def affine_T(n):
                for g in range(G):
                    act.wait_ge(s_nT[n], g + 1)
                    A(LNT[:, cs(g)], ps[:, g % 2, :], ACT.Identity, bias=BETA, scale=GAMMA).then_inc(s_lnT[n], 1)

            act.wait_ge(ld_small, 16 * 12)
            affine_T(0)
            for g in range(G):
                act.wait_ge(s_kv, 2 * g + 2)
                nc.scalar.copy(V[:, cs(g)], ps[:, 5 + 2 * (g % 2), :]).then_inc(s_v, 1)
            for g in range(G):
                act.wait_ge(s_attT, g + 1)
                nc.scalar.copy(QP[:, cs(g)], ps[:, g % 2, :]).then_inc(s_attTs, 1)
            for g in range(G):
                inv_std(1, g, 1e-6)
            affine_T(1)
            for g in range(G + 1):
                if g < G:
                    for c in range(NF):
                        act.wait_ge(s_f1, NF * g + c + 1)
                        if g >= 2 and c == 0:
                            act.wait_ge(s_f2, g - 1)
                        A(HT[:, g % 2, c, :], ps[:, 4 + c, :], ACT.Gelu, bias=B1C[:, c:c + 1]).then_inc(s_g1, 1)
                if g >= 1:
                    act.wait_ge(s_f2, g)
                    A(LNT[:, cs(g - 1)], ps[:, 2 + (g - 1) % 2, :], ACT.Gelu).then_inc(s_g2, 1)
            for g in range(G):
                act.wait_ge(s_cT, g + 1)
                nc.scalar.copy(CTXT[:, cs(g)], ps[:, g % 2, :]).then_inc(s_cTs, 1)

            def square(t, g, done_mm, bias):
                act.wait_ge(done_mm, g + 1)
                if t == 1:
                    act.wait_ge(s_lo[0], g + 1)
                A(QP[:, cs(g)], ps[:, 2 + g % 2, :], ACT.Square, bias=bias).then_inc(s_sq[t], 1)

            def head_inv_std(t, g):
                act.wait_ge(s_var[t], g + 1)
                A(KP[:, cs(g)], ps[:, 6 + g % 2, :], ACT.Ln, bias=1e-6).then_inc(s_lv[t], 1)
                act.wait_ge(s_lv[t], g + 1)
                A(KP[:, cs(g)], KP[:, cs(g)], ACT.Exp, scale=-0.5).then_inc(s_rs[t], 1)

            def parts(t, g, src, rest):
                act.wait_ge((s_aff[0], s_qh)[t], g + 1)
                if g >= 2:
                    act.wait_ge(s_scr[t], 16 * (g - 1))
                if t == 1 and g < 2:
                    act.wait_ge(s_scr[0], 16 * G)
                nc.scalar.copy(PART[:, g % 2, 0, :], src[:, cs(g)]).then_inc(s_hi[t], 1)
                act.wait_ge(s_r1[t], g + 1)
                nc.scalar.copy(PART[:, g % 2, 1, :], rest[:, cs(g)]).then_inc(s_mid[t], 1)

            for g in range(G + 1):
                if g < G:
                    square(0, g, s_kc, KBC)
                    head_inv_std(0, g)
                if g >= 1:
                    parts(0, g - 1, V, QP)
            for g in range(G):
                inv_std(2, g, 1e-5)
            for g in range(G):
                act.wait_ge(s_nT[2], g + 1)
                nc.scalar.copy(LNT[:, cs(g)], ps[:, g % 2, :]).then_inc(s_lnT[2], 1)
            for g in range(G):
                square(1, g, s_qc, QBC)
                head_inv_std(1, g)
            for g in range(G):
                parts(1, g, ADD, KP)
            def negate_max(b):
                act.wait_ge(s_mT, b + 1)
                if b >= 2:
                    act.wait_ge(s_mrow[b % 2], 32 * (b // 2))
                A(NEGM[:, b % 2, :], ps[0:H, 7, 0:P], ACT.Copy, scale=-1.0).then_inc(s_negm, 1)

            negate_max(0)
            negate_max(1)
            for u in range(4 * B):
                b, r = divmod(u, 4)
                act.wait_ge(s_sc, u + 1)
                if u >= 4:
                    act.wait_ge(s_pv, u - 3)
                A(EXPS[:, u % 4, :], ps[:, 2 + u % 3, :], ACT.Exp).then_inc(s_exp, 1)
                if r == 0 and 1 <= b and b + 1 < B:
                    negate_max(b + 1)
            for g in range(G):
                act.wait_ge(s_oT, g + 1)
                nc.scalar.copy(QP[:, cs(g)], ps[:, g % 2, :]).then_inc(s_oTs, 1)
            for g in range(G):
                act.wait_ge(s_y2, g + 1)
                b = slice(g * GB, (g + 1) * GB)
                A(lnv[:, 3, b], mv[:, 3, b, 1], ACT.Ln, bias=1e-5).then_inc(s_elv, 1)
                act.wait_ge(s_elv, g + 1)
                A(rstd[:, 3, b], lnv[:, 3, b], ACT.Exp, scale=-0.5).then_inc(s_ers, 1)
            for n in range((SLOTS + 3) // 4):
                act.wait_ge(s_xsT, n + 1)
                k = min(4, SLOTS - 4 * n)
                nc.scalar.copy(XST[:, 4 * n * P:(4 * n + k) * P], ps[:, n % 2, 0:k * P]).then_inc(s_xst, 1)
            act.wait_ge(s_cnt, 1)
            act.sem_inc(s_ha, 1)
            act.wait_ge(ld_exp, 16 * 3)
            reg = [act.value_load(cnti[0:1, 1, h:h + 1], min_val=0, max_val=SLOTS) for h in range(NE + 1)]
            for h in range(NE):
                with act.Fori(reg[h], reg[h + 1]) as t:
                    act.wait_ge(s_h, t + 1)
                    act.wait_ge(s_ye, t + 1)
                    for c in range(NF):
                        last = A(HE[:, c, :], ps[:, 0, c * P:(c + 1) * P], ACT.Relu, bias=EB1[:, h, c:c + 1])
                    last.then_inc(s_ha, 1)
                    act.wait_ge(s_emv, t + 1)
                    A(emv[:, 2:3], emv[:, 1:2], ACT.Ln, bias=1e-5).then_inc(s_elv, 1)
                    act.wait_ge(s_elv, t + G + 1)
                    A(emv[:, 3:4], emv[:, 2:3], ACT.Exp, scale=-0.5).then_inc(s_ers, 1)

        @block.vector
        def _(dve):
            ts, tt, stt = nc.vector.tensor_scalar, nc.vector.tensor_tensor, nc.vector.scalar_tensor_tensor
            n_st = [0]

            def mean_var(src, n, g, done):
                for j in range(GB):
                    b = g * GB + j
                    nc.vector.bn_stats(st[:, b, :], src(b)).then_inc(s_st, 1)
                    n_st[0] += 1
                for j in range(GB):
                    b = g * GB + j
                    dve.wait_ge(s_st, n_st[0] - GB + 1 + j)
                    last = nc.vector.bn_aggr(mv[:, n, b, :], st[:, b, :])
                last.then_inc(done, 1)

            def normalise(dst, src, n, g, ready, done):
                dve.wait_ge(ready, g + 1)
                for j in range(GB):
                    b = g * GB + j
                    last = ts(dst(b), src(b), mv[:, n, b, 0:1], rstd[:, n, b:b + 1], ALU.subtract, ALU.mult)
                last.then_inc(done, 1)

            for g in range(G):
                dve.wait_ge(ld_x[g], 16)
                mean_var(lambda b: blk(X, b), 0, g, s_mv[0])
            for g in range(G):
                normalise(lambda b: blk(N, b), lambda b: blk(X, b), 0, g, s_rstd[0], s_norm[0])
            for g in range(G):
                dve.wait_ge(s_q, g + 1)
                ts(QP[:, cs(g)], ps[:, 2 + g % 2, :], 0.0, STAB, ALU.max, ALU.add).then_inc(s_qp, 1)
                dve.wait_ge(s_kv, 2 * g + 1)
                ts(KP[:, cs(g)], ps[:, 4 + 2 * (g % 2), :], 0.0, STAB, ALU.max, ALU.add).then_inc(s_kp, 1)
            dve.wait_ge(ld_const, 16)
            for g in range(G):
                dve.wait_ge(s_kvs, g + 1)
                b = slice(g * GB, (g + 1) * GB)
                tt(KVS[:, b, 0:P], bank_rows(g % 2), K["same_head"][:, None, :].to_broadcast([P, GB, P]), ALU.mult)
                tt(KVS[:, b, P:P + H], ps[:, 2 + g % 2, 0:GB][:, :, None].to_broadcast([P, GB, H]),
                   head_mask[:, None, :].to_broadcast([P, GB, H]), ALU.mult).then_inc(s_kvsm, 1)
            for g in range(G):
                dve.wait_ge(s_num, g + 1)
                for i in range(2):
                    o = ps[:, 4 + 2 * (g % 2) + i, :].rearrange("p (b e) -> p b e", b=2)
                    b = slice(g * GB + 2 * i, g * GB + 2 * i + 2)
                    nc.vector.reciprocal(RD[:, b, :], o[:, :, P:P + H]).then_inc(s_rd1, 1)
                for j in range(GB):
                    b = g * GB + j
                    dve.wait_ge(s_rd1, 2 * g + j // 2 + 1)
                    o = ps[:, 4 + 2 * (g % 2) + j // 2, (j % 2) * 2 * P:(j % 2) * 2 * P + P]
                    last = tt(blk(KP, b).rearrange("p (h d) -> p h d", d=HD), o.rearrange("p (h d) -> p h d", d=HD),
                              RD[:, b, :][:, :, None].to_broadcast([P, H, HD]), ALU.mult)
                last.then_inc(s_att, 1)
            for g in range(G):
                dve.wait_ge(s_ao, g + 1)
                tt(ADD[:, cs(g)], ps[:, 2 + g % 2, :], X[:, cs(g)], ALU.add).then_inc(s_add, 1)
                dve.wait_ge(s_add, g + 1)
                mean_var(lambda b: blk(ADD, b), 1, g, s_mv[1])
            for g in range(G):
                normalise(lambda b: blk(N, b), lambda b: blk(ADD, b), 1, g, s_rstd[1], s_norm[1])
            for g in range(G):
                dve.wait_ge(s_g2, g + 1)
                dve.wait_ge(s_2x, g + 1)
                tt(LNT[:, cs(g)], LNT[:, cs(g)], X[:, cs(g)], ALU.add).then_inc(s_y, 1)
                dve.wait_ge(s_y, g + 1)
                mean_var(lambda b: blk(LNT, b), 2, g, s_mv[2])

            def head_norm(t, g, bias):
                dve.wait_ge(s_rs[t], g + 1)
                stt(out=V[:, cs(g)], in0=ps[:, 2 + g % 2, :], scalar=bias, in1=KP[:, cs(g)],
                    op0=ALU.add, op1=ALU.mult).then_inc(s_n8[t], 1)

            dve.wait_ge(s_va1, 1)
            for g in range(G):
                dve.wait_ge(s_v2, g + 1)
                for j in range(GB):
                    last = tt(VAUG[:, g * GB + j, :, 0:HD], ps[:, 4 + g % 2, j * P:(j + 1) * P].rearrange("p (h d) -> p h d", d=HD),
                              rows[:, 1, :].rearrange("p (h d) -> p h d", d=HD), ALU.add)
                last.then_inc(s_vaug, 1)
                head_norm(0, g, KBC)
            for g in range(G):
                normalise(lambda b: blk(N, b), lambda b: blk(LNT, b), 2, g, s_rstd[2], s_norm[2])
            for g in range(G):
                dve.wait_ge(s_lo[0], g + 1)
                head_norm(1, g, QBC)
            for g in range(G):
                dve.wait_ge(s_rot, g + 1)
                tt(QP[:, cs(g)].rearrange("p (b s) -> p b s", b=GB), bank_rows(4 + g % 2),
                   K["sin"][:, None, :].to_broadcast([P, GB, P]), ALU.mult).then_inc(s_t2, 1)
                dve.wait_ge(s_t1, g + 1)
                dve.wait_ge(s_t2, g + 1)
                tt(ADD[:, cs(g)], ADD[:, cs(g)], QP[:, cs(g)], ALU.add).then_inc(s_qh, 1)

            def maxima(u):
                b, r = divmod(u, 4)
                par, half = r % 2, r // 2
                dve.wait_ge(s_sm, u + 1)
                if r == 0 and b >= 2:
                    dve.wait_ge(s_mT, b - 1)
                c = par * 8 + half * 4
                nc.vector.tensor_reduce(M[:, b % 2, c:c + 4], bank_rows(u % 2), AX.X, ALU.max).then_inc(s_max, 1)

            def attention_rows(b):
                dve.wait_ge(s_pv, 4 * (b + 1))
                o = ps[:, 5 + b % 2, 0:H * 9].rearrange("p (h d) -> p h d", d=9)
                nc.vector.reciprocal(RD[:, b, :], o[:, :, HD]).then_inc(s_rd2, 1)
                dve.wait_ge(s_rd2, b + 1)
                tt(blk(KP, b).rearrange("p (h d) -> p h d", d=HD), o[:, :, 0:HD],
                   RD[:, b, :][:, :, None].to_broadcast([P, H, HD]), ALU.mult).then_inc(s_on, 1)

            for u in range(8):
                maxima(u)
            for u in range(4 * B):
                b, r = divmod(u, 4)
                if u + 8 < 4 * B:
                    maxima(u + 8)
                if r == 2 and b >= 1:
                    attention_rows(b - 1)
            attention_rows(B - 1)
            for g in range(G):
                dve.wait_ge(s_pr, g + 1)
                dve.wait_ge(s_x1b, g + 1)
                tt(N[:, cs(g)], ps[:, 2 + g % 2, :], X[:, cs(g)], ALU.add).then_inc(s_y, 1)
                dve.wait_ge(s_y, G + g + 1)
                mean_var(lambda b: blk(N, b), 3, g, s_y2)
            dve.wait_ge(s_x2id, 1)
            for g in range(G):
                normalise(lambda b: X2[:, b, 0:P], lambda b: blk(N, b), 3, g, s_ers, s_x2)
            steps = [0]

            def step(ins):
                steps[0] += 1
                ins.then_inc(s_rt, 1)
                dve.wait_ge(s_rt, steps[0])

            dve.wait_ge(s_x2, G)
            SUM, MAG, NEAR, UP, NEG, HH = (rt[:, i, :] for i in range(6))
            step(tt(SUM, X2[:, :, 0], X2[:, :, 1], ALU.add))
            step(stt(out=MAG, in0=SUM, scalar=-1.0, in1=SUM, op0=ALU.mult, op1=ALU.max))
            step(nc.vector.tensor_copy(rti[:, 0, :], MAG))
            step(nc.vector.tensor_copy(NEAR, rti[:, 0, :]))
            step(tt(UP, NEAR, MAG, ALU.is_gt))
            step(tt(NEAR, NEAR, UP, ALU.subtract))
            step(ts(NEG, SUM, 0.0, -2.0, ALU.is_lt, ALU.mult))
            step(stt(out=HH, in0=NEG, scalar=1.0, in1=NEAR, op0=ALU.add, op1=ALU.mult))
            step(ts(HH, HH, 32.0, None, ALU.add))
            step(nc.vector.tensor_copy(rti[:, 0, :], HH))
            step(ts(rti[:, 1, :], rti[:, 0, :], NE - 1, None, ALU.bitwise_and))
            step(nc.vector.tensor_copy(HH, rti[:, 1, :]))
            tt(OH[:, :, :], HH[:, :, None].to_broadcast([P, B, NE]), expert_no[:, None, :].to_broadcast([P, B, NE]),
               ALU.is_equal).then_inc(s_oh, 1)
            dve.wait_ge(s_rank, 1)
            step(nc.vector.tensor_copy(tot[:, 0, :, :], ps[:, 7, P:2 * P].rearrange("p (b e) -> p b e", e=NE)))
            a = 0
            for d in (1, 2, 4, 8):
                nc.vector.tensor_copy(tot[:, 1 - a, 0:d, :], tot[:, a, 0:d, :])
                step(tt(tot[:, 1 - a, d:B, :], tot[:, a, d:B, :], tot[:, a, 0:B - d, :], ALU.add))
                a = 1 - a
            step(ts(cnt[:, 0, :], tot[:, a, B - 1, :], P - 1.0, None, ALU.add))
            step(nc.vector.tensor_copy(cnti[:, 0, 0:NE], cnt[:, 0, :]))
            step(ts(cnti[:, 0, 0:NE], cnti[:, 0, 0:NE], 7, None, ALU.arith_shift_right))
            step(nc.vector.tensor_copy(cnt[:, 0, :], cnti[:, 0, 0:NE]))
            step(ts(cnt[:, 0, :], cnt[:, 0, :], 1.0, None, ALU.max))
            nc.vector.memset(starts[:, :, :], 0.0)
            step(nc.vector.tensor_copy(cnt[:, 1, :], cnt[:, 0, :]))
            c = 1
            for d in (1, 2, 4):
                nc.vector.tensor_copy(cnt[:, 3 - c, 0:d], cnt[:, c, 0:d])
                step(tt(cnt[:, 3 - c, d:NE], cnt[:, c, d:NE], cnt[:, c, 0:NE - d], ALU.add))
                c = 3 - c
            step(nc.vector.tensor_copy(starts[:, 0, 1:NE + 1], cnt[:, c, :]))
            nc.vector.tensor_copy(cnti[:, 1, :], starts[:, 0, :]).then_inc(s_cnt, 1)
            step(ts(starts[:, 1, :], starts[:, 0, :], float(P), None, ALU.mult))
            step(tt(rank[:, :, :], ps[:, 7, 0:P].rearrange("p (b e) -> p b e", e=NE),
                    starts[:, 1, 0:NE][:, None, :].to_broadcast([P, B, NE]), ALU.add))
            step(tt(rank[:, 1:B, :], rank[:, 1:B, :], tot[:, a, 0:B - 1, :], ALU.add))
            step(tt(rank[:, :, :], rank[:, :, :], OH[:, :, :], ALU.mult))
            step(nc.vector.tensor_reduce(HH, rank[:, :, :], AX.X, ALU.add))
            nc.vector.tensor_copy(posu[:, :], HH).then_inc(s_pos, 1)
            dve.wait_ge(ld_exp, 16 * 3)
            dve.wait_ge(s_cnt, 1)
            dve.sem_inc(s_hb, 1)
            dve.sem_inc(s_res, 1)
            reg = [dve.value_load(cnti[0:1, 1, h:h + 1], min_val=0, max_val=SLOTS) for h in range(NE + 1)]
            for h in range(NE):
                with dve.Fori(reg[h], reg[h + 1]) as t:
                    dve.wait_ge(s_h, t + 1)
                    dve.wait_ge(s_ye, t + 1)
                    for c in range(NF):
                        last = ts(HE[:, NF + c, :], ps[:, 1, c * P:(c + 1) * P], EB1[:, (h + 1) % NE, c:c + 1], 0.0, ALU.add, ALU.max)
                    last.then_inc(s_hb, 1)
                    dve.wait_ge(s_ye, t + 2)
                    dve.wait_ge(s_xb, t + 1)
                    stt(out=RES[:, 0, :], in0=ps[:, 2, 0:P], scalar=0.5, in1=XBS[:, :], op0=ALU.mult, op1=ALU.add).then_inc(s_res, 1)
                    dve.wait_ge(s_res, t + 2)
                    nc.vector.bn_stats(est[:, :], RES[:, 0, :]).then_inc(s_est, 1)
                    dve.wait_ge(s_cnt, 1)
                    dve.wait_ge(s_est, t + 1)
                    nc.vector.bn_aggr(emv[:, 0:2], est[:, :]).then_inc(s_emv, 1)
                    dve.wait_ge(s_ers, t + G + 1)
                    dve.wait_ge(s_out, t * 16 + 16)
                    ts(OUTN[:, :], RES[:, 0, :], emv[:, 0:1], emv[:, 3:4], ALU.subtract, ALU.mult).then_inc(s_outn, 1)

        @block.gpsimd
        def _(pool):
            ts, tt = nc.gpsimd.tensor_scalar, nc.gpsimd.tensor_tensor
            nc.gpsimd.memset(VAUG[:, :, :, :], 1.0).then_inc(s_va1, 1)
            nc.gpsimd.memset(fill[:, 0:P], 0.0).then_inc(s_fillm, 1)
            nc.gpsimd.memset(fill[:, P:ROW], NO_TOKEN).then_inc(s_fillm, 1)
            pool.wait_ge(s_fillm, 2)
            pool.dma_start(sorted_scr.rearrange("(s p) r -> p s r", p=P),
                           fill[:, None, :].to_broadcast([P, SLOTS, ROW])).then_inc(s_out, 16)
            for g in range(G):
                pool.wait_ge(s_add, g + 1)
                tt(X[:, cs(g)], X[:, cs(g)], ADD[:, cs(g)], ALU.add).then_inc(s_2x, 1)

            def low(t, g, src, rest):
                pool.wait_ge(s_hi[t], g + 1)
                tt(rest[:, cs(g)], src[:, cs(g)], PART[:, g % 2, 0, :], ALU.subtract).then_inc(s_r1[t], 1)
                pool.wait_ge(s_mid[t], g + 1)
                tt(PART[:, g % 2, 2, :], rest[:, cs(g)], PART[:, g % 2, 1, :], ALU.subtract).then_inc(s_lo[t], 1)

            for g in range(G):
                pool.wait_ge(s_n8[0], g + 1)
                ts(V[:, cs(g)], V[:, cs(g)], KNW, KNB, ALU.mult, ALU.add).then_inc(s_aff[0], 1)
                low(0, g, V, QP)
            for g in range(G):
                pool.wait_ge(s_norm[2], g + 1)
                tt(rows_of(X, g), rows_of(N, g), rows[:, 2, :][:, None, :].to_broadcast([P, GB, P]), ALU.add).then_inc(s_x1b, 1)
            for g in range(G):
                pool.wait_ge(s_n8[1], g + 1)
                ts(V[:, cs(g)], V[:, cs(g)], QNW, QNB, ALU.mult, ALU.add).then_inc(s_aff[1], 1)
                pool.wait_ge(s_aff[1], g + 1)
                tt(rows_of(ADD, g), rows_of(V, g), K["cos"][:, None, :].to_broadcast([P, GB, P]), ALU.mult).then_inc(s_t1, 1)
            for g in range(G):
                low(1, g, ADD, KP)
            pool.wait_ge(s_att, G)
            pool.wait_ge(s_num, G)
            nc.gpsimd.tensor_copy(X2[:, :, P:ROW], token_no[:, :, None].to_broadcast([P, B, ROW - P])).then_inc(s_x2id, 1)
            pool.wait_ge(ld_eb2, 16 * NE)
            pool.wait_ge(s_qc, G)
            tt(EB2P[:, 0:NE - 1, :], EB2[:, 0:NE - 1, :], EB2[:, 1:NE, :], ALU.add)
            tt(EB2P[:, NE - 1, :], EB2[:, NE - 1, :], EB2[:, 0, :], ALU.add).then_inc(s_eb2, 1)
            pool.wait_ge(s_eb2, 1)
            ts(EB2P[:, :, :], EB2P[:, :, :], 0.5, 1.0, ALU.mult, ALU.mult).then_inc(s_eb2, 1)
            pool.wait_ge(s_pos, 1)
            pool.wait_ge(s_x2, G)
            pool.wait_ge(s_out, 16)
            for b in range(B):
                pool.indirect_dma_start(sorted_scr, bass.IndirectOffsetOnAxis(ap=posu[:, b:b + 1], axis=0),
                                        X2[:, b, :], None).then_inc(s_sort, 16)
            pool.wait_ge(s_xs, 16)
            pool.wait_ge(s_cnt, 1)
            pool.wait_ge(s_eb2, 2)
            last_row = pool.to_reg(NTOK - 1)
            reg = [pool.value_load(cnti[0:1, 1, h:h + 1], min_val=0, max_val=SLOTS) for h in range(NE + 1)]
            for h in range(NE):
                with pool.Fori(reg[h], reg[h + 1]) as t:
                    pool.wait_ge(s_res, t + 1)
                    pool.wait_ge(s_h, t + 1)
                    tt(XBS[:, :], XS[:, bass.ds(t, 1), 0:P].rearrange("p a e -> p (a e)"), EB2P[:, h, :], ALU.add).then_inc(s_xb, 1)
                    pool.wait_ge(s_out, t * 16 + 16)
                    nc.gpsimd.tensor_copy(tok_u[:, :], XS[:, bass.ds(t, 1), P:P + 1].rearrange("p a e -> p (a e)")).then_inc(s_tok, 1)
                    pool.wait_ge(s_cnt, 1)
                    pool.wait_ge(s_tok, t + 1)
                    pool.wait_ge(s_outn, t + 1)
                    pool.indirect_dma_start(out_rows, bass.IndirectOffsetOnAxis(ap=tok_u[:, 0:1], axis=0),
                                            OUTN[:, :], None, bounds_check=last_row, oob_is_err=False).then_inc(s_out, 16)
            pool.wait_ge(s_cnt, 1)
            pool.wait_ge(s_out, reg[NE] * 16 + 16)


_INS = ['x', 'ctx_1024', 'L0_attn_gamma1', 'L0_attn_beta1', 'L0_attn_wq', 'L0_attn_wk', 'L0_attn_wv', 'L0_attn_wo',
        'L0_attn_w1', 'L0_attn_b1', 'L0_attn_w2', 'L0_attn_b2', 'L0_xattn_q_w', 'L0_xattn_q_b', 'L0_xattn_kv_w',
        'L0_xattn_kv_b', 'L0_xattn_qn_w', 'L0_xattn_qn_b', 'L0_xattn_kn_w', 'L0_xattn_kn_b', 'L0_xattn_out_w',
        'L0_xattn_out_b', 'L0_ffn_W1', 'L0_ffn_b1', 'L0_ffn_W2', 'L0_ffn_b2']
_PER_HEAD = ('L0_xattn_qn_w', 'L0_xattn_qn_b', 'L0_xattn_kn_w', 'L0_xattn_kn_b')


def kernel(**inputs):
    import numpy as _np
    import concourse.bacc as _bacc
    from concourse import mybir as _mybir
    from concourse.bass_utils import run_bass_kernel_spmd as _run

    nc = _bacc.Bacc("TRN2", target_bir_lowering=False, num_devices=1)
    arrays, args = {}, []

    def give(name, a):
        arrays[name] = a
        args.append(nc.dram_tensor(name, a.shape, _mybir.dt.from_np(a.dtype), kind="ExternalInput").ap())

    for name in _INS:
        a = _np.ascontiguousarray(inputs[name])
        if name in _PER_HEAD:
            a = _np.ascontiguousarray(_np.tile(a, H).reshape(P, 1))
        if name in ('L0_attn_b1', 'L0_ffn_b1'):
            a = _np.ascontiguousarray(_np.moveaxis(a.reshape(a.shape[:-1] + (NF, P)), -1, 0))
        give(f"in_{name}_dram", a)
    give("in_constants_dram", constants())
    give("in_ones_dram", _np.ones((1, H // 2, NTOK), _mybir.dt.np(BF16)))
    args.append(nc.dram_tensor("out_0_dram", (B, P, P), F32, kind="ExternalOutput").ap())
    decoder_layer(nc, *args)
    r = _run(nc, [arrays], core_ids=[0])
    return r.results[0]["out_0_dram"]
```

```python
from contextlib import ExitStack

import numpy as np

import concourse.bass as bass
from concourse import mybir

F32 = mybir.dt.float32
BF16 = mybir.dt.bfloat16
I32 = mybir.dt.int32
U32 = mybir.dt.uint32
ALU = mybir.AluOpType
ACT = mybir.ActivationFunctionType
AX = mybir.AxisListType

P = 128
B = 16
H = 16
HD = 8
GB = 4
G = B // GB
W = GB * P
NTOK = B * P
NF = 4
NE = 8
SLOTS = B + NE - 1
ROW = P + 4
STAB = 0.001
LN_EXP = "natural_log_exp_and_others"
NO_TOKEN = 65536.0
TERMS_K = (0, 0, 0, 1, 1, 2)
TERMS_Q = (0, 1, 2, 0, 1, 0)
KROWS = HD * len(TERMS_K)
AHEAD = 3
RING = 4
TILE = 32
HALF = 64

CONSTS = ("ident", "center", "mean8", "same_head", "rotate", "cos", "sin", "lower", "ones", "row0")


def constants():
    i = np.arange(P)
    same = (i[:, None] // HD == i[None, :] // HD).astype(np.float32)
    d = i % 64 // 8
    feature = 16 * (i % 8) + 8 * (i // 64) + d
    permute = (i[:, None] == feature[None, :]).astype(np.float32)
    freq = 1.0 / 10000.0 ** (np.arange(0, HD, 2, dtype=np.float32) / HD)
    ang = np.arange(P, dtype=np.float32)[None, :] * freq[d // 2][:, None]
    scale = HD ** -0.5
    rot = np.zeros((P, P), np.float32)
    rot[i[1::2], i[0::2]] = -1.0
    rot[i[0::2], i[1::2]] = 1.0
    row0 = np.zeros((P, P), np.float32)
    row0[0] = 1.0
    mats = {
        "ident": np.eye(P), "center": (np.eye(P) - same / HD) @ permute,
        "mean8": permute.T @ (same / HD) @ permute, "same_head": same, "rotate": permute.T @ rot @ permute, "cos": np.cos(ang) * scale, "sin": np.sin(ang) * scale,
        "lower": (i[:, None] < i[None, :]), "ones": np.ones((P, P)), "row0": row0,
    }
    small = np.zeros((P, 64), np.float32)
    small[:, 0:H] = i[:, None] // HD == np.arange(H)[None, :]
    small[:, 16:16 + NE] = np.arange(NE)[None, :]
    small[:, 32:48] = i[:, None] + P * np.arange(B)[None, :]
    return np.ascontiguousarray(np.concatenate([mats[n].astype(np.float32) for n in CONSTS] + [small], 1))


def decoder_layer(nc, x, ctx_in, attn_w, w1, w2, col_params, row_params, xw, eW1, eb1, eW2, eb2, consts, ones_row,
                  out):
    packed_scr = [nc.dram_tensor(f"{n}_packed_scratch", (2, len(TERMS_K), P // 2, NTOK), BF16).ap() for n in "kq"]
    sorted_scr = nc.dram_tensor("sorted_scratch", (SLOTS * P, ROW), F32).ap()
    out_rows = out.rearrange("b s e -> (b s) e")

    with ExitStack() as ctx:
        def sb(name, shape, dt=F32):
            return ctx.enter_context(nc.sbuf_tensor(name, shape, dt))

        def sem(name):
            return ctx.enter_context(nc.semaphore(name))

        X = sb("X", [P, NTOK])
        N = sb("N", [P, NTOK])
        LNT = sb("LNT", [P, NTOK])
        QP = sb("QP", [P, NTOK])
        KP = sb("KP", [P, NTOK])
        V = sb("V", [P, NTOK])
        ADD = sb("ADD", [P, NTOK])
        CTX = sb("CTX", [P, NTOK])
        KVS = sb("KVS", [P, B, P + H + 4])
        PART = sb("PART", [P, 2, 3, W], BF16)
        QPK = sb("QPK", [P, H // 2, NTOK], BF16)
        KPK = sb("KPK", [P, H // 2, NTOK], BF16)
        EW1 = sb("EW1", [P, NE, NF * P])
        EW2 = sb("EW2", [P, NE, NF, P])
        VA = sb("VA", [P, B * H * (HD + 1) + TILE])
        VAUG = VA[:, 0:B * H * (HD + 1)].rearrange("p (b h d) -> p b h d", b=B, h=H)
        OT = V[:, 0:2 * W].rearrange("p (r w) -> p r w", r=2)
        EXPS = CTX[:, :].rearrange("p (r w) -> p r w", r=4)
        qpk_f = QPK[:, :, :].rearrange("p i t -> p (i t)").bitcast(F32)
        kpk_f = KPK[:, :, :].rearrange("p i t -> p (i t)").bitcast(F32)
        HT = qpk_f[:, 0:4096].rearrange("p (r c w) -> p r c w", r=2, c=NF)
        CTXT = qpk_f[:, 4096:6144]
        X2 = KVS[:, :, 0:ROW]
        XS = kpk_f[:, 0:(SLOTS + 1) * ROW].rearrange("p (s r) -> p s r", s=SLOTS + 1)
        XST = qpk_f[:, 0:SLOTS * P]
        HE = kpk_f[:, (SLOTS + 1) * ROW:(SLOTS + 1) * ROW + 2 * NF * P].rearrange("p (c t) -> p c t", c=2 * NF)

        C = sb("C", [P, len(CONSTS) * P + 64])
        K = {n: C[:, i * P:(i + 1) * P] for i, n in enumerate(CONSTS)}
        head_mask = C[:, len(CONSTS) * P:len(CONSTS) * P + H]
        expert_no = C[:, len(CONSTS) * P + 16:len(CONSTS) * P + 16 + NE]
        token_no = C[:, len(CONSTS) * P + 32:len(CONSTS) * P + 48]
        WA = sb("WA", [P, 4, P])
        WQ, WK, WV, WO = (WA[:, n, :] for n in range(4))
        W1 = sb("W1", [P, NF * P])
        W2 = sb("W2", [P, NF, P])
        XW = sb("XW", [P, 4, P])
        XWT = sb("XWT", [P, 4, P])
        cols = sb("cols", [P, 18])
        GAMMA, BETA, QB, KB, QNW, QNB, KNW, KNB = (cols[:, i:i + 1] for i in range(8))
        QBC, KBC = cols[:, 16:17], cols[:, 17:18]
        B1C = cols[:, 8:12]
        rows = sb("rows", [P, 3, P])
        EB1 = sb("EB1", [P, NE, NF])
        EB2 = LNT[:, NE * P:2 * NE * P].rearrange("p (e d) -> p e d", e=NE)
        EB2P = LNT[:, 0:NE * P].rearrange("p (e d) -> p e d", e=NE)
        st = sb("st", [P, B, 6])
        mv = sb("mv", [P, 4, B, 2])
        lnv = sb("lnv", [P, 4, B])
        rstd = sb("rstd", [P, 4, B])
        RD = sb("RD", [P, B, H])
        M = sb("M", [P, RING, H])
        NEGM = sb("NEGM", [H, RING, P], BF16)
        rt = sb("rt", [P, 8, B])
        rti = sb("rti", [P, 2, B], I32)
        posu = sb("posu", [P, B], U32)
        OH = V[:, 0:P].rearrange("p (b e) -> p b e", e=NE)
        tot = V[:, P:3 * P].rearrange("p (a b e) -> p a b e", a=2, e=NE)
        rank = V[:, 3 * P:4 * P].rearrange("p (b e) -> p b e", e=NE)
        cnt = sb("cnt", [P, 4, NE])
        cnti = sb("cnti", [P, 2, NE + 1], I32)
        starts = sb("starts", [P, 2, NE + 1])
        fill = sb("fill", [P, ROW])
        XBS = ADD[:, 0:P]
        RES = ADD[:, P:3 * P].rearrange("p (a e) -> p a e", a=2)
        OUTN = ADD[:, 3 * P:4 * P]
        est = sb("est", [P, 6])
        emv = sb("emv", [P, 4])
        tok_f = sb("tok_f", [P, 2])
        tok_u = sb("tok_u", [P, 1], U32)
        ps = ctx.enter_context(nc.psum_tensor("ps", [P, 8, W], F32))

        def cs(g):
            return slice(g * W, (g + 1) * W)

        def blk(t, b):
            return t[:, b * P:(b + 1) * P]

        def rows_of(t, g):
            return t[:, cs(g)].rearrange("p (b e) -> p b e", b=GB)

        def bank_rows(bank):
            return ps[:, bank, :].rearrange("p (b e) -> p b e", b=GB)

        ld_x = [sem(f"ld_x{g}") for g in range(G)]
        ld_const = sem("ld_const")
        ld_attn = sem("ld_attn"); ld_ffn = sem("ld_ffn")
        ld_rows = sem("ld_rows")
        ld_ctx = sem("ld_ctx")
        ld_xw = sem("ld_xw")
        ld_small = sem("ld_small")
        ld_exp = sem("ld_exp")
        ld_eb2 = sem("ld_eb2")
        ld_ones = sem("ld_ones")
        s_mv = [sem(f"s_mv{n}") for n in range(3)]
        s_lnv = [sem(f"s_lnv{n}") for n in range(3)]
        s_rstd = [sem(f"s_rstd{n}") for n in range(3)]
        s_st = sem("s_st")
        s_norm = [sem(f"s_norm{n}") for n in range(3)]
        s_nT = [sem(f"s_nT{n}") for n in range(3)]
        s_lnT = [sem(f"s_lnT{n}") for n in range(3)]
        s_q = sem("s_q"); s_kv = sem("s_kv")
        s_qp = sem("s_qp"); s_kp = sem("s_kp"); s_v = sem("s_v")
        s_kvs = sem("s_kvs"); s_kvsm = sem("s_kvsm")
        s_num = sem("s_num"); s_rd1 = sem("s_rd1"); s_att = sem("s_att")
        s_attT = sem("s_attT"); s_attTs = sem("s_attTs")
        s_ao = sem("s_ao"); s_add = sem("s_add"); s_2x = sem("s_2x")
        s_f1 = sem("s_f1"); s_g1 = sem("s_g1")
        s_f2 = sem("s_f2"); s_g2 = sem("s_g2"); s_y = sem("s_y")
        s_x1b = sem("s_x1b")
        s_prep = sem("s_prep"); s_xwt = sem("s_xwt")
        s_cT = sem("s_cT"); s_cTs = sem("s_cTs")
        s_kc = sem("s_kc"); s_v2 = sem("s_v2"); s_va1 = sem("s_va1"); s_vaug = sem("s_vaug")
        s_sq = [sem("s_sq_k"), sem("s_sq_q")]
        s_var = [sem("s_var_k"), sem("s_var_q")]
        s_lv = [sem("s_lv_k"), sem("s_lv_q")]
        s_rs = [sem("s_rs_k"), sem("s_rs_q")]
        s_n8 = [sem("s_n8_k"), sem("s_n8_q")]
        s_aff = [sem("s_aff_k"), sem("s_aff_q")]
        s_hi = [sem("s_hi_k"), sem("s_hi_q")]
        s_r1 = [sem("s_r1_k"), sem("s_r1_q")]
        s_mid = [sem("s_mid_k"), sem("s_mid_q")]
        s_lo = [sem("s_lo_k"), sem("s_lo_q")]
        s_scr = [sem("s_scr_k"), sem("s_scr_q")]
        s_pack = [[sem(f"s_pack_k{g}") for g in range(G)], [sem(f"s_pack_q{g}") for g in range(G)]]
        s_qc = sem("s_qc"); s_rot = sem("s_rot"); s_t1 = sem("s_t1"); s_t2 = sem("s_t2"); s_qh = sem("s_qh")
        s_sm = sem("s_sm"); s_max = sem("s_max")
        s_mT = sem("s_mT"); s_negm = sem("s_negm")
        s_mrow = [sem(f"s_mrow{n}") for n in range(RING)]
        s_sc = sem("s_sc"); s_exp = sem("s_exp"); s_pv = sem("s_pv")
        s_otc = sem("s_otc"); s_otT = sem("s_otT")
        s_rd2 = sem("s_rd2"); s_on = sem("s_on")
        s_oT = sem("s_oT"); s_oTs = sem("s_oTs"); s_pr = sem("s_pr"); s_y2 = sem("s_y2"); s_x2 = sem("s_x2")
        s_x2id = sem("s_x2id")
        s_rt = sem("s_rt")
        s_oh = sem("s_oh"); s_rank = sem("s_rank")
        s_pos = sem("s_pos"); s_cnt = sem("s_cnt")
        s_fillm = sem("s_fillm"); s_sort = sem("s_sort"); s_xs = sem("s_xs")
        s_xsT = sem("s_xsT"); s_xst = sem("s_xst")
        s_eb2 = sem("s_eb2")
        s_h = sem("s_h"); s_ha = sem("s_ha"); s_hb = sem("s_hb"); s_ye = sem("s_ye")
        s_xb = sem("s_xb"); s_res = sem("s_res"); s_est = sem("s_est"); s_emv = sem("s_emv")
        s_elv = sem("s_elv"); s_ers = sem("s_ers"); s_outn = sem("s_outn")
        s_tokf = sem("s_tokf"); s_tok = sem("s_tok"); s_out = sem("s_out")

        block = ctx.enter_context(nc.Block())

        @block.sync
        def _(sp):
            xv = x.rearrange("b s e -> s b e")
            for g in range(G):
                sp.dma_start(rows_of(X, g), xv[:, g * GB:(g + 1) * GB, :]).then_inc(ld_x[g], 16)
            sp.dma_start(C[:, :], consts).then_inc(ld_const, 16)
            sp.dma_start(cols[:, 0:12], col_params).then_inc(ld_small, 16)
            sp.dma_start(WA[:, :, :], attn_w.rearrange("n e f -> e n f")).then_inc(ld_attn, 16)
            sp.dma_start(W1[:, :], w1).then_inc(ld_ffn, 16)
            sp.dma_start(W2[:, :, :], w2.rearrange("(c p) e -> p c e", p=P)).then_inc(ld_ffn, 16)
            sp.dma_start(rows[:, :, :], row_params[None, :, :].to_broadcast([P, 3, P])).then_inc(ld_rows, 16)
            sp.dma_start(CTX[:, :].rearrange("p (b e) -> p b e", b=B), ctx_in.rearrange("b s e -> s b e")).then_inc(ld_ctx, 16)
            sp.dma_start(XW[:, :, :], xw.rearrange("n o i -> o n i")).then_inc(ld_xw, 16)
            sp.dma_start(EB1[:, :, :], eb1).then_inc(ld_exp, 16)
            sp.dma_start(EW1[:, :, :], eW1.rearrange("e d f -> d e f")).then_inc(ld_exp, 16)
            sp.dma_start(EW2[:, :, :, :], eW2.rearrange("e (c p) d -> p e c d", p=P)).then_inc(ld_exp, 16)
            for r in (KROWS, HALF + KROWS):
                sp.dma_start(KPK[r:r + 1, :, :], ones_row).then_inc(ld_ones, 16)
            for t, (pack, terms) in enumerate(((KPK, TERMS_K), (QPK, TERMS_Q))):
                scr = packed_scr[t]
                for g in range(G):
                    for n in range(3):
                        sp.wait_ge((s_hi, s_mid, s_lo)[n][t], g + 1)
                        for m in [m for m, part in enumerate(terms) if part == n]:
                            sp.dma_start(scr[:, m, :, cs(g)], PART[:, g % 2, n, :]).then_inc(s_scr[t], 16)
                    sp.wait_ge(s_scr[t], 16 * len(terms) * (g + 1))
                    if t == 1 and g == 0:
                        sp.wait_ge(s_kc, G)
                        sp.wait_ge(s_v2, G)
                        sp.wait_ge(s_f2, G)
                    for r in range(2):
                        sp.dma_start(pack[HALF * r:HALF * r + KROWS, :, cs(g)],
                                     scr[r].rearrange("m (d i) s -> (m d) i s", d=HD)[:, :, cs(g)]).then_inc(s_pack[t][g], 16)
            sp.wait_ge(s_qc, G)
            sp.dma_start(EB2, eb2[None, :, :].to_broadcast([P, NE, P])).then_inc(ld_eb2, 16)
            for b in range(B):
                sp.wait_ge(s_negm, b + 1)
                sp.dma_start(QPK[KROWS:HALF + KROWS + 1:HALF, :, b * P:(b + 1) * P],
                             NEGM[:, b % RING, :]).then_inc(s_mrow[b % RING], 16)
            sp.wait_ge(s_sort, 16 * B)
            sp.wait_ge(s_sc, 4 * B)
            sp.dma_start(XS[:, 1:SLOTS + 1, :], sorted_scr.rearrange("(s p) r -> p s r", p=P)).then_inc(s_xs, 16)

        @block.tensor
        def _(pe):
            mm = nc.tensor.matmul

            def transposes(bank, src, g, done, k=GB):
                for j in range(k):
                    last = nc.tensor.transpose(ps[:, bank, j * P:(j + 1) * P], blk(src, g * GB + j), K["ident"])
                last.then_inc(done, 1)

            pe.wait_ge(ld_const, 16)

            def norm_T(n):
                for g in range(G):
                    pe.wait_ge(s_norm[n], g + 1)
                    if g >= 2:
                        pe.wait_ge(s_lnT[n], g - 1)
                    transposes(g % 2, N, g, s_nT[n])

            norm_T(0)
            pe.wait_ge(ld_attn, 16)
            for g in range(G):
                pe.wait_ge(s_lnT[0], g + 1)
                if g >= 2:
                    pe.wait_ge(s_qp, g - 1)
                mm(ps[:, 2 + g % 2, :], WQ, LNT[:, cs(g)], start=True, stop=True).then_inc(s_q, 1)
                if g >= 2:
                    pe.wait_ge(s_kp, g - 1)
                    pe.wait_ge(s_v, g - 1)
                for i in range(2):
                    for j in range(GB):
                        last = mm(ps[:, 4 + 2 * (g % 2) + i, j * P:(j + 1) * P],
                                  blk(LNT, g * GB + j), (WK, WV)[i], start=True, stop=True)
                    last.then_inc(s_kv, 1)
            for g in range(G):
                pe.wait_ge(s_kp, g + 1)
                pe.wait_ge(s_v, g + 1)
                if g == 0:
                    pe.wait_ge(s_lnT[0], G)
                    pe.wait_ge(s_qp, G)
                if g >= 2:
                    pe.wait_ge(s_kvsm, g - 1)
                for j in range(GB):
                    b = g * GB + j
                    mm(ps[:, g % 2, j * P:(j + 1) * P], blk(KP, b), blk(V, b), start=True, stop=True)
                    last = mm(ps[:, 2 + g % 2, j:j + 1], blk(KP, b), K["ones"][:, 0:1], start=True, stop=True)
                last.then_inc(s_kvs, 1)
            for g in range(G):
                pe.wait_ge(s_kvsm, g + 1)
                if g == 0:
                    pe.wait_ge(s_kp, G)
                    pe.wait_ge(s_v, G)
                if g >= 2:
                    pe.wait_ge(s_att, g - 1)
                for j in range(GB):
                    b = g * GB + j
                    last = mm(ps[:, 4 + 2 * (g % 2) + j // 2, (j % 2) * 2 * P:(j % 2) * 2 * P + P + H],
                              blk(QP, b), KVS[:, b, 0:P + H], start=True, stop=True)
                last.then_inc(s_num, 1)
            for g in range(G):
                pe.wait_ge(s_att, g + 1)
                if g == 0:
                    pe.wait_ge(s_kvsm, G)
                if g >= 2:
                    pe.wait_ge(s_attTs, g - 1)
                transposes(g % 2, KP, g, s_attT)
            for g in range(G):
                pe.wait_ge(s_attTs, g + 1)
                if g >= 2:
                    pe.wait_ge(s_add, g - 1)
                for j in range(GB):
                    last = mm(ps[:, 2 + g % 2, j * P:(j + 1) * P], blk(QP, g * GB + j), WO, start=True, stop=True)
                last.then_inc(s_ao, 1)
            pe.wait_ge(s_attTs, G)
            norm_T(1)

            def ffn1(g):
                pe.wait_ge(s_lnT[1], g + 1)
                for c in range(NF):
                    if g >= 1:
                        pe.wait_ge(s_g1, NF * (g - 1) + c + 1)
                    mm(ps[:, 4 + c, :], W1[:, c * P:(c + 1) * P], LNT[:, cs(g)], start=True, stop=True).then_inc(s_f1, 1)

            def ffn2(g):
                pe.wait_ge(s_g1, NF * (g + 1))
                if g == 0:
                    pe.wait_ge(s_add, G)
                if g >= 2:
                    pe.wait_ge(s_g2, g - 1)
                for j in range(GB):
                    o = ps[:, 2 + g % 2, j * P:(j + 1) * P]
                    for c in range(NF):
                        mm(o, HT[:, g % 2, c, j * P:(j + 1) * P], W2[:, c, :], start=(c == 0), stop=False)
                    last = mm(o, K["row0"], rows[:, 0, :], start=False, stop=True)
                last.then_inc(s_f2, 1)

            pe.wait_ge(s_att, G)
            pe.wait_ge(ld_ffn, 32)
            pe.wait_ge(ld_rows, 16)
            for g in range(G + 1):
                if g < G:
                    ffn1(g)
                if g >= 1:
                    ffn2(g - 1)
            pe.wait_ge(ld_xw, 16)
            pe.wait_ge(ld_small, 16)
            pe.wait_ge(s_g1, NF * G)
            for n, right in enumerate((K["center"], K["center"], K["ident"], K["ident"])):
                mm(ps[:, 7, n * P:(n + 1) * P], XW[:, n, :], right, start=True, stop=True)
            mm(ps[:, 6, 0:1], K["center"], QB, start=True, stop=True)
            mm(ps[:, 6, 1:2], K["center"], KB, start=True, stop=True).then_inc(s_prep, 1)
            pe.wait_ge(ld_ctx, 16)
            pe.wait_ge(s_lnT[1], G)
            for g in range(G):
                if g >= 2:
                    pe.wait_ge(s_cTs, g - 1)
                transposes(g % 2, CTX, g, s_cT)
            for g in range(G):
                pe.wait_ge(s_cTs, g + 1)
                if g == 0:
                    pe.wait_ge(s_g2, G)
                if g >= 2:
                    pe.wait_ge(s_n8[0], g - 1)
                    pe.wait_ge(s_sq[0], g - 1)
                if g == 0:
                    pe.wait_ge(s_xwt, 2)
                mm(ps[:, 2 + g % 2, :], XWT[:, 1, :], CTXT[:, cs(g)], start=True, stop=True).then_inc(s_kc, 1)
                if g == 0:
                    pe.wait_ge(s_g1, NF * G)
                if g >= 2:
                    pe.wait_ge(s_vaug, g - 1)
                for j in range(GB):
                    last = mm(ps[:, 4 + g % 2, j * P:(j + 1) * P], blk(CTXT, g * GB + j), XWT[:, 2, :], start=True, stop=True)
                last.then_inc(s_v2, 1)
                pe.wait_ge(s_sq[0], g + 1)
                if g >= 2:
                    pe.wait_ge(s_lv[0], g - 1)
                mm(ps[:, 6 + g % 2, :], K["mean8"], QP[:, cs(g)], start=True, stop=True).then_inc(s_var[0], 1)
            pe.wait_ge(s_cTs, G)
            norm_T(2)
            for g in range(G):
                pe.wait_ge(s_lnT[2], g + 1)
                if g == 0:
                    pe.wait_ge(s_n8[0], G)
                if g >= 2:
                    pe.wait_ge(s_n8[1], g - 1)
                mm(ps[:, 2 + g % 2, :], XWT[:, 0, :], LNT[:, cs(g)], start=True, stop=True).then_inc(s_qc, 1)
                pe.wait_ge(s_sq[1], g + 1)
                if g == 0:
                    pe.wait_ge(s_lv[0], G)
                if g >= 2:
                    pe.wait_ge(s_lv[1], g - 1)
                mm(ps[:, 6 + g % 2, :], K["mean8"], QP[:, cs(g)], start=True, stop=True).then_inc(s_var[1], 1)
            for g in range(G):
                pe.wait_ge(s_aff[1], g + 1)
                if g == 0:
                    pe.wait_ge(s_vaug, G)
                if g >= 2:
                    pe.wait_ge(s_t2, g - 1)
                mm(ps[:, 4 + g % 2, :], K["rotate"], V[:, cs(g)], start=True, stop=True).then_inc(s_rot, 1)

            def unit(u):
                b, r = divmod(u, 4)
                return b, r % 2, r // 2

            def scores_for_max(u):
                b, par, half = unit(u)
                if u % (4 * GB) == 0:
                    pe.wait_ge(s_pack[0][b // GB], 32)
                    pe.wait_ge(s_pack[1][b // GB], 32)
                if u == 0:
                    pe.wait_ge(s_lnT[2], G)
                if u >= 2:
                    pe.wait_ge(s_max, u - 1)
                t = slice(b * P, (b + 1) * P)
                for j in range(4):
                    last = mm(ps[:, u % 2, j * P:(j + 1) * P], QPK[HALF * par:HALF * par + KROWS, 4 * half + j, t],
                              KPK[HALF * par:HALF * par + KROWS, 4 * half + j, t], start=True, stop=True)
                last.then_inc(s_sm, 1)

            def max_T(b):
                pe.wait_ge(s_max, 4 * (b + 1))
                if b == 0:
                    pe.wait_ge(s_lv[1], G)
                if b >= 1:
                    pe.wait_ge(s_negm, b)
                nc.tensor.transpose(ps[0:H, 7, 0:P], M[:, b % RING, :], K["ident"]).then_inc(s_mT, 1)

            def scores(u):
                b, par, half = unit(u)
                if u % 4 == 0:
                    pe.wait_ge(s_mrow[b % RING], 16 * (b // RING + 1))
                if u == 0:
                    pe.wait_ge(ld_ones, 32)
                    pe.wait_ge(s_n8[1], G)
                    pe.wait_ge(s_t2, G)
                if u >= 2:
                    pe.wait_ge(s_exp, u - 1)
                t = slice(b * P, (b + 1) * P)
                for j in range(4):
                    last = mm(ps[:, 2 + u % 2, j * P:(j + 1) * P], KPK[HALF * par:HALF * par + KROWS + 1, 4 * half + j, t],
                              QPK[HALF * par:HALF * par + KROWS + 1, 4 * half + j, t], start=True, stop=True)
                last.then_inc(s_sc, 1)

            def times_v(u):
                b, par, half = unit(u)
                pe.wait_ge(s_exp, u + 1)
                if u % 4 == 0 and b >= 2:
                    pe.wait_ge(s_otc, b - 1)
                if u == 0:
                    pe.wait_ge(s_vaug, G)
                for j in range(4):
                    c = (b * H + 2 * (4 * half + j) + par) * (HD + 1)
                    last = mm(ps[TILE * (u % 4):TILE * (u % 4 + 1), 5 + b % 2, j * P:(j + 1) * P], VA[:, c:c + TILE],
                              EXPS[:, u % 4, j * P:(j + 1) * P], start=True, stop=True)
                last.then_inc(s_pv, 1)

            def results_T(b):
                pe.wait_ge(s_otc, b + 1)
                if b == 0:
                    pe.wait_ge(s_t2, G)
                if b >= 1:
                    pe.wait_ge(s_on, b)
                if b >= GB and b % GB == 0:
                    pe.wait_ge(s_oTs, b // GB)
                if b > GB and b % GB == 1:
                    pe.wait_ge(s_y, G + b // GB)
                for j in range(4):
                    last = nc.tensor.transpose(ps[:, 4, j * P:(j + 1) * P], OT[:, b % 2, j * P:(j + 1) * P], K["ident"])
                last.then_inc(s_otT, 1)

            def rows_T(g):
                pe.wait_ge(s_on, GB * (g + 1))
                transposes(4, KP, g, s_oT)

            def project(g):
                pe.wait_ge(s_oTs, g + 1)
                pe.wait_ge(s_on, min(GB * (g + 1) + 1, B))
                for j in range(GB):
                    last = mm(ps[:, 4, j * P:(j + 1) * P], blk(QP, g * GB + j), XWT[:, 3, :], start=True, stop=True)
                last.then_inc(s_pr, 1)

            for b in range(AHEAD):
                for r in range(4):
                    scores_for_max(4 * b + r)
                max_T(b)
            for u in range(4 * B):
                b, r = divmod(u, 4)
                scores(u)
                if b + AHEAD < B:
                    scores_for_max(u + 4 * AHEAD)
                if u >= 2:
                    times_v(u - 2)
                if r == 0 and 1 <= b and b + AHEAD - 1 < B:
                    max_T(b + AHEAD - 1)
                if r == 1 and b > GB and b % GB == 1:
                    rows_T(b // GB - 1)
                if r == 1 and b > GB and b % GB == 2:
                    project(b // GB - 1)
                if r == 3 and b >= 1:
                    results_T(b - 1)
            times_v(4 * B - 2)
            times_v(4 * B - 1)
            results_T(B - 1)
            rows_T(G - 1)
            project(G - 1)
            pe.wait_ge(s_oh, 1)
            pe.wait_ge(s_negm, B)
            oh = OH[:, :, :].rearrange("p b e -> p (b e)")
            mm(ps[:, 7, 0:P], K["lower"], oh, start=True, stop=True)
            mm(ps[:, 7, P:2 * P], K["ones"], oh, start=True, stop=True).then_inc(s_rank, 1)
            pe.wait_ge(s_xs, 16)
            pe.wait_ge(s_max, 4 * B)
            for n in range((SLOTS + 3) // 4):
                if n >= 2:
                    pe.wait_ge(s_xst, n - 1)
                k = min(4, SLOTS - 4 * n)
                for j in range(k):
                    last = nc.tensor.transpose(ps[:, n % 2, j * P:(j + 1) * P], XS[:, 1 + 4 * n + j, 0:P], K["ident"])
                last.then_inc(s_xsT, 1)
            pe.wait_ge(s_xst, (SLOTS + 3) // 4)
            pe.wait_ge(s_exp, 4 * B)
            pe.wait_ge(s_on, B)
            pe.wait_ge(ld_exp, 16 * 3)
            reg = [pe.value_load(cnti[0:1, 1, h:h + 1], min_val=0, max_val=SLOTS) for h in range(NE + 1)]
            for h in range(NE):
                with pe.Fori(reg[h], reg[h + 1]) as t:
                    for c in range(2 * NF):
                        e = (h + c // NF) % NE
                        last = mm(ps[:, c // 2, (c % 2) * P:(c % 2 + 1) * P], EW1[:, e, (c % NF) * P:(c % NF + 1) * P],
                                  XST[:, bass.ds(t * P, P)], start=True, stop=True)
                        if c % 2 == 1:
                            last.then_inc(s_h, 1)
                    pe.wait_ge(s_res, t + 1)
                    for c in range(2 * NF):
                        e = (h + c // NF) % NE
                        if c % 2 == 0:
                            pe.wait_ge(s_ha if c < NF else s_hb, t * 2 + c % NF // 2 + 1)
                        last = mm(ps[:, 4, 0:P], HE[:, c, :], EW2[:, e, c % NF, :], start=(c == 0), stop=(c == 2 * NF - 1))
                    last.then_inc(s_ye, 1)

        @block.scalar
        def _(act):
            A = nc.scalar.activation

            def inv_std(n, g, eps):
                act.wait_ge(s_mv[n], g + 1)
                b = slice(g * GB, (g + 1) * GB)
                A(lnv[:, n, b], mv[:, n, b, 1], ACT.Ln, bias=eps).then_inc(s_lnv[n], 1)
                act.wait_ge(s_lnv[n], g + 1)
                A(rstd[:, n, b], lnv[:, n, b], ACT.Exp, scale=-0.5).then_inc(s_rstd[n], 1)

            nc.scalar.preload_act_table_set(LN_EXP)
            for g in range(G):
                inv_std(0, g, 1e-6)

            def affine_T(n):
                for g in range(G):
                    act.wait_ge(s_nT[n], g + 1)
                    A(LNT[:, cs(g)], ps[:, g % 2, :], ACT.Identity, bias=BETA, scale=GAMMA).then_inc(s_lnT[n], 1)

            act.wait_ge(ld_small, 16)
            affine_T(0)
            for g in range(G):
                act.wait_ge(s_kv, 2 * g + 2)
                nc.scalar.copy(V[:, cs(g)], ps[:, 5 + 2 * (g % 2), :]).then_inc(s_v, 1)
            for g in range(G):
                act.wait_ge(s_attT, g + 1)
                nc.scalar.copy(QP[:, cs(g)], ps[:, g % 2, :]).then_inc(s_attTs, 1)
            for g in range(G):
                inv_std(1, g, 1e-6)
            affine_T(1)
            for g in range(G + 1):
                if g < G:
                    for c in range(NF):
                        act.wait_ge(s_f1, NF * g + c + 1)
                        if g >= 2 and c == 0:
                            act.wait_ge(s_f2, g - 1)
                        A(HT[:, g % 2, c, :], ps[:, 4 + c, :], ACT.Gelu, bias=B1C[:, c:c + 1]).then_inc(s_g1, 1)
                if g >= 1:
                    act.wait_ge(s_f2, g)
                    A(LNT[:, cs(g - 1)], ps[:, 2 + (g - 1) % 2, :], ACT.Gelu).then_inc(s_g2, 1)
            act.wait_ge(s_prep, 1)
            nc.scalar.copy(XWT[:, :, :].rearrange("p n e -> p (n e)"), ps[:, 7, :]).then_inc(s_xwt, 1)
            nc.scalar.copy(cols[:, 16:18], ps[:, 6, 0:2]).then_inc(s_xwt, 1)
            nc.scalar.preload_act_table_set(LN_EXP)
            for g in range(G):
                act.wait_ge(s_cT, g + 1)
                nc.scalar.copy(CTXT[:, cs(g)], ps[:, g % 2, :]).then_inc(s_cTs, 1)

            def square(t, g, done_mm, bias):
                act.wait_ge(done_mm, g + 1)
                if t == 1:
                    act.wait_ge(s_lo[0], g + 1)
                A(QP[:, cs(g)], ps[:, 2 + g % 2, :], ACT.Square, bias=bias).then_inc(s_sq[t], 1)

            def head_inv_std(t, g):
                act.wait_ge(s_var[t], g + 1)
                A(KP[:, cs(g)], ps[:, 6 + g % 2, :], ACT.Ln, bias=1e-6).then_inc(s_lv[t], 1)
                act.wait_ge(s_lv[t], g + 1)
                A(KP[:, cs(g)], KP[:, cs(g)], ACT.Exp, scale=-0.5).then_inc(s_rs[t], 1)

            def parts(t, g, src, rest):
                act.wait_ge((s_aff[0], s_qh)[t], g + 1)
                if g >= 2:
                    act.wait_ge(s_scr[t], 16 * len(TERMS_K) * (g - 1))
                if t == 1 and g < 2:
                    act.wait_ge(s_scr[0], 16 * len(TERMS_K) * G)
                nc.scalar.copy(PART[:, g % 2, 0, :], src[:, cs(g)]).then_inc(s_hi[t], 1)
                act.wait_ge(s_r1[t], g + 1)
                nc.scalar.copy(PART[:, g % 2, 1, :], rest[:, cs(g)]).then_inc(s_mid[t], 1)

            for g in range(G + 1):
                if g < G:
                    square(0, g, s_kc, KBC)
                    head_inv_std(0, g)
                if g >= 1:
                    parts(0, g - 1, V, QP)
            for g in range(G):
                inv_std(2, g, 1e-5)
            for g in range(G):
                act.wait_ge(s_nT[2], g + 1)
                nc.scalar.copy(LNT[:, cs(g)], ps[:, g % 2, :]).then_inc(s_lnT[2], 1)
            for g in range(G):
                square(1, g, s_qc, QBC)
                head_inv_std(1, g)
            for g in range(G):
                parts(1, g, ADD, KP)
            def negate_max(b):
                act.wait_ge(s_mT, b + 1)
                if b >= RING:
                    act.wait_ge(s_mrow[b % RING], 16 * (b // RING))
                A(NEGM[:, b % RING, :], ps[0:H, 7, 0:P], ACT.Copy, scale=-1.0).then_inc(s_negm, 1)

            for b in range(AHEAD):
                negate_max(b)
            def copy_oT(g):
                act.wait_ge(s_oT, g + 1)
                nc.scalar.copy(QP[:, cs(g)], ps[:, 4, :]).then_inc(s_oTs, 1)

            def inv_std_x2(g):
                act.wait_ge(s_y2, g + 1)
                b = slice(g * GB, (g + 1) * GB)
                A(lnv[:, 3, b], mv[:, 3, b, 1], ACT.Ln, bias=1e-5).then_inc(s_elv, 1)
                act.wait_ge(s_elv, g + 1)
                A(rstd[:, 3, b], lnv[:, 3, b], ACT.Exp, scale=-0.5).then_inc(s_ers, 1)

            for u in range(4 * B):
                b, r = divmod(u, 4)
                act.wait_ge(s_sc, u + 1)
                if u >= 4:
                    act.wait_ge(s_pv, u - 3)
                A(EXPS[:, u % 4, :], ps[:, 2 + u % 2, :], ACT.Exp).then_inc(s_exp, 1)
                if r == 0 and 1 <= b and b + AHEAD - 1 < B:
                    negate_max(b + AHEAD - 1)
                if r == 1 and b > GB and b % GB == 1:
                    copy_oT(b // GB - 1)
                if r == 1 and b > GB and b % GB == 3:
                    inv_std_x2(b // GB - 1)
            copy_oT(G - 1)
            inv_std_x2(G - 1)
            for n in range((SLOTS + 3) // 4):
                act.wait_ge(s_xsT, n + 1)
                k = min(4, SLOTS - 4 * n)
                nc.scalar.copy(XST[:, 4 * n * P:(4 * n + k) * P], ps[:, n % 2, 0:k * P]).then_inc(s_xst, 1)
            act.wait_ge(s_cnt, 1)
            nc.scalar.preload_act_table_set(LN_EXP)
            act.wait_ge(ld_exp, 16 * 3)
            reg = [act.value_load(cnti[0:1, 1, h:h + 1], min_val=0, max_val=SLOTS) for h in range(NE + 1)]

            def slot_inv_std(t):
                act.wait_ge(s_emv, t + 1)
                A(emv[:, 2:3], emv[:, 1:2], ACT.Ln, bias=1e-5).then_inc(s_elv, 1)
                act.wait_ge(s_elv, t + G + 1)
                A(emv[:, 3:4], emv[:, 2:3], ACT.Exp, scale=-0.5).then_inc(s_ers, 1)

            for h in range(NE):
                with act.Fori(reg[h], reg[h + 1]) as t:
                    for k in range(2):
                        act.wait_ge(s_h, t * 4 + k + 1)
                        for c in (2 * k, 2 * k + 1):
                            last = A(HE[:, c, :], ps[:, k, (c % 2) * P:(c % 2 + 1) * P], ACT.Relu, bias=EB1[:, h, c:c + 1])
                        last.then_inc(s_ha, 1)
                        if k == 0:
                            slot_inv_std(t)
            slot_inv_std(reg[NE])

        @block.vector
        def _(dve):
            ts, tt, stt = nc.vector.tensor_scalar, nc.vector.tensor_tensor, nc.vector.scalar_tensor_tensor
            n_st = [0]

            def mean_var(src, n, g, done):
                for j in range(GB):
                    b = g * GB + j
                    nc.vector.bn_stats(st[:, b, :], src(b)).then_inc(s_st, 1)
                    n_st[0] += 1
                for j in range(GB):
                    b = g * GB + j
                    dve.wait_ge(s_st, n_st[0] - GB + 1 + j)
                    last = nc.vector.bn_aggr(mv[:, n, b, :], st[:, b, :])
                last.then_inc(done, 1)

            def normalise(dst, src, n, g, ready, done):
                dve.wait_ge(ready, g + 1)
                for j in range(GB):
                    b = g * GB + j
                    last = ts(dst(b), src(b), mv[:, n, b, 0:1], rstd[:, n, b:b + 1], ALU.subtract, ALU.mult)
                last.then_inc(done, 1)

            for g in range(G):
                dve.wait_ge(ld_x[g], 16)
                mean_var(lambda b: blk(X, b), 0, g, s_mv[0])
            for g in range(G):
                normalise(lambda b: blk(N, b), lambda b: blk(X, b), 0, g, s_rstd[0], s_norm[0])
            for g in range(G):
                dve.wait_ge(s_q, g + 1)
                ts(QP[:, cs(g)], ps[:, 2 + g % 2, :], 0.0, STAB, ALU.max, ALU.add).then_inc(s_qp, 1)
                dve.wait_ge(s_kv, 2 * g + 1)
                ts(KP[:, cs(g)], ps[:, 4 + 2 * (g % 2), :], 0.0, STAB, ALU.max, ALU.add).then_inc(s_kp, 1)
            dve.wait_ge(ld_const, 16)
            for g in range(G):
                dve.wait_ge(s_kvs, g + 1)
                b = slice(g * GB, (g + 1) * GB)
                tt(KVS[:, b, 0:P], bank_rows(g % 2), K["same_head"][:, None, :].to_broadcast([P, GB, P]), ALU.mult)
                tt(KVS[:, b, P:P + H], ps[:, 2 + g % 2, 0:GB][:, :, None].to_broadcast([P, GB, H]),
                   head_mask[:, None, :].to_broadcast([P, GB, H]), ALU.mult).then_inc(s_kvsm, 1)
            for g in range(G):
                dve.wait_ge(s_num, g + 1)
                for i in range(2):
                    o = ps[:, 4 + 2 * (g % 2) + i, :].rearrange("p (b e) -> p b e", b=2)
                    b = slice(g * GB + 2 * i, g * GB + 2 * i + 2)
                    nc.vector.reciprocal(RD[:, b, :], o[:, :, P:P + H]).then_inc(s_rd1, 1)
                for j in range(GB):
                    b = g * GB + j
                    dve.wait_ge(s_rd1, 2 * g + j // 2 + 1)
                    o = ps[:, 4 + 2 * (g % 2) + j // 2, (j % 2) * 2 * P:(j % 2) * 2 * P + P]
                    last = tt(blk(KP, b).rearrange("p (h d) -> p h d", d=HD), o.rearrange("p (h d) -> p h d", d=HD),
                              RD[:, b, :][:, :, None].to_broadcast([P, H, HD]), ALU.mult)
                last.then_inc(s_att, 1)
            for g in range(G):
                dve.wait_ge(s_ao, g + 1)
                tt(ADD[:, cs(g)], ps[:, 2 + g % 2, :], X[:, cs(g)], ALU.add).then_inc(s_add, 1)
                dve.wait_ge(s_add, g + 1)
                mean_var(lambda b: blk(ADD, b), 1, g, s_mv[1])
            for g in range(G):
                normalise(lambda b: blk(N, b), lambda b: blk(ADD, b), 1, g, s_rstd[1], s_norm[1])
            for g in range(G):
                dve.wait_ge(s_g2, g + 1)
                dve.wait_ge(s_2x, g + 1)
                tt(LNT[:, cs(g)], LNT[:, cs(g)], X[:, cs(g)], ALU.add).then_inc(s_y, 1)
                dve.wait_ge(s_y, g + 1)
                mean_var(lambda b: blk(LNT, b), 2, g, s_mv[2])

            def head_norm(t, g, bias):
                dve.wait_ge(s_rs[t], g + 1)
                stt(out=V[:, cs(g)], in0=ps[:, 2 + g % 2, :], scalar=bias, in1=KP[:, cs(g)],
                    op0=ALU.add, op1=ALU.mult).then_inc(s_n8[t], 1)

            dve.wait_ge(s_va1, 1)
            dve.wait_ge(ld_rows, 16)
            dve.wait_ge(s_xwt, 2)
            for g in range(G):
                dve.wait_ge(s_v2, g + 1)
                for j in range(GB):
                    last = tt(VAUG[:, g * GB + j, :, 0:HD], ps[:, 4 + g % 2, j * P:(j + 1) * P].rearrange("p (h d) -> p h d", d=HD),
                              rows[:, 1, :].rearrange("p (h d) -> p h d", d=HD), ALU.add)
                last.then_inc(s_vaug, 1)
                head_norm(0, g, KBC)
            for g in range(G):
                normalise(lambda b: blk(N, b), lambda b: blk(LNT, b), 2, g, s_rstd[2], s_norm[2])
            for g in range(G):
                dve.wait_ge(s_lo[0], g + 1)
                head_norm(1, g, QBC)
            for g in range(G):
                dve.wait_ge(s_rot, g + 1)
                tt(QP[:, cs(g)].rearrange("p (b s) -> p b s", b=GB), bank_rows(4 + g % 2),
                   K["sin"][:, None, :].to_broadcast([P, GB, P]), ALU.mult).then_inc(s_t2, 1)
                dve.wait_ge(s_t1, g + 1)
                dve.wait_ge(s_t2, g + 1)
                tt(ADD[:, cs(g)], ADD[:, cs(g)], QP[:, cs(g)], ALU.add).then_inc(s_qh, 1)

            def maxima(u):
                b, r = divmod(u, 4)
                par, half = r % 2, r // 2
                dve.wait_ge(s_sm, u + 1)
                if r == 0 and b >= RING:
                    dve.wait_ge(s_mT, b - RING + 1)
                c = par * 8 + half * 4
                nc.vector.tensor_reduce(M[:, b % RING, c:c + 4], bank_rows(u % 2), AX.X, ALU.max).then_inc(s_max, 1)

            def copy_results(b):
                dve.wait_ge(s_pv, 4 * (b + 1))
                if b >= 2:
                    dve.wait_ge(s_otT, b - 1)
                nc.vector.tensor_copy(OT[:, b % 2, :], ps[:, 5 + b % 2, :]).then_inc(s_otc, 1)

            def attention_rows(b):
                dve.wait_ge(s_otT, b + 1)
                o = ps[:, 4, :].rearrange("p (h d) -> p h d", h=H)
                nc.vector.reciprocal(RD[:, b, :], o[:, :, HD]).then_inc(s_rd2, 1)
                dve.wait_ge(s_rd2, b + 1)
                tt(blk(KP, b).rearrange("p (h d) -> p h d", d=HD), o[:, :, 0:HD],
                   RD[:, b, :][:, :, None].to_broadcast([P, H, HD]), ALU.mult).then_inc(s_on, 1)

            def add_x1(g):
                dve.wait_ge(s_pr, g + 1)
                dve.wait_ge(s_x1b, g + 1)
                tt(N[:, cs(g)], ps[:, 4, :], X[:, cs(g)], ALU.add).then_inc(s_y, 1)
                dve.wait_ge(s_y, G + g + 1)
                mean_var(lambda b: blk(N, b), 3, g, s_y2)

            def normalise_x2(g):
                if g == 0:
                    dve.wait_ge(s_x2id, 1)
                normalise(lambda b: X2[:, b, 0:P], lambda b: blk(N, b), 3, g, s_ers, s_x2)

            for u in range(4 * AHEAD):
                maxima(u)
            for u in range(4 * B):
                b, r = divmod(u, 4)
                if u + 4 * AHEAD < 4 * B:
                    maxima(u + 4 * AHEAD)
                if r == 0 and b >= 2:
                    attention_rows(b - 2)
                if r == 2 and b > GB and b % GB == 2:
                    add_x1(b // GB - 1)
                if r == 2 and b > GB and b % GB == 3:
                    normalise_x2(b // GB - 1)
                if r == 2 and b >= 1:
                    copy_results(b - 1)
            attention_rows(B - 2)
            copy_results(B - 1)
            attention_rows(B - 1)
            add_x1(G - 1)
            normalise_x2(G - 1)
            steps = [0]

            def step(ins):
                steps[0] += 1
                ins.then_inc(s_rt, 1)
                dve.wait_ge(s_rt, steps[0])

            dve.wait_ge(s_x2, G)
            SUM, MAG, NEAR, UP, NEG, HH = (rt[:, i, :] for i in range(6))
            step(tt(SUM, X2[:, :, 0], X2[:, :, 1], ALU.add))
            step(stt(out=MAG, in0=SUM, scalar=-1.0, in1=SUM, op0=ALU.mult, op1=ALU.max))
            step(nc.vector.tensor_copy(rti[:, 0, :], MAG))
            step(nc.vector.tensor_copy(NEAR, rti[:, 0, :]))
            step(tt(UP, NEAR, MAG, ALU.is_gt))
            step(tt(NEAR, NEAR, UP, ALU.subtract))
            step(ts(NEG, SUM, 0.0, -2.0, ALU.is_lt, ALU.mult))
            step(stt(out=HH, in0=NEG, scalar=1.0, in1=NEAR, op0=ALU.add, op1=ALU.mult))
            step(ts(HH, HH, 32.0, None, ALU.add))
            step(nc.vector.tensor_copy(rti[:, 0, :], HH))
            step(ts(rti[:, 1, :], rti[:, 0, :], NE - 1, None, ALU.bitwise_and))
            step(nc.vector.tensor_copy(HH, rti[:, 1, :]))
            tt(OH[:, :, :], HH[:, :, None].to_broadcast([P, B, NE]), expert_no[:, None, :].to_broadcast([P, B, NE]),
               ALU.is_equal).then_inc(s_oh, 1)
            dve.wait_ge(s_rank, 1)
            step(nc.vector.tensor_copy(tot[:, 0, :, :], ps[:, 7, P:2 * P].rearrange("p (b e) -> p b e", e=NE)))
            a = 0
            for d in (1, 2, 4, 8):
                nc.vector.tensor_copy(tot[:, 1 - a, 0:d, :], tot[:, a, 0:d, :])
                step(tt(tot[:, 1 - a, d:B, :], tot[:, a, d:B, :], tot[:, a, 0:B - d, :], ALU.add))
                a = 1 - a
            step(ts(cnt[:, 0, :], tot[:, a, B - 1, :], P - 1.0, None, ALU.add))
            step(nc.vector.tensor_copy(cnti[:, 0, 0:NE], cnt[:, 0, :]))
            step(ts(cnti[:, 0, 0:NE], cnti[:, 0, 0:NE], 7, None, ALU.arith_shift_right))
            step(nc.vector.tensor_copy(cnt[:, 0, :], cnti[:, 0, 0:NE]))
            step(ts(cnt[:, 0, :], cnt[:, 0, :], 1.0, None, ALU.max))
            nc.vector.memset(starts[:, :, :], 0.0)
            step(nc.vector.tensor_copy(cnt[:, 1, :], cnt[:, 0, :]))
            c = 1
            for d in (1, 2, 4):
                nc.vector.tensor_copy(cnt[:, 3 - c, 0:d], cnt[:, c, 0:d])
                step(tt(cnt[:, 3 - c, d:NE], cnt[:, c, d:NE], cnt[:, c, 0:NE - d], ALU.add))
                c = 3 - c
            step(nc.vector.tensor_copy(starts[:, 0, 1:NE + 1], cnt[:, c, :]))
            nc.vector.tensor_copy(cnti[:, 1, :], starts[:, 0, :]).then_inc(s_cnt, 1)
            step(ts(starts[:, 1, :], starts[:, 0, :], float(P), None, ALU.mult))
            step(tt(rank[:, :, :], ps[:, 7, 0:P].rearrange("p (b e) -> p b e", e=NE),
                    starts[:, 1, 0:NE][:, None, :].to_broadcast([P, B, NE]), ALU.add))
            step(tt(rank[:, 1:B, :], rank[:, 1:B, :], tot[:, a, 0:B - 1, :], ALU.add))
            step(tt(rank[:, :, :], rank[:, :, :], OH[:, :, :], ALU.mult))
            step(nc.vector.tensor_reduce(HH, rank[:, :, :], AX.X, ALU.add))
            nc.vector.tensor_copy(posu[:, :], HH).then_inc(s_pos, 1)
            dve.wait_ge(ld_exp, 16 * 3)
            dve.wait_ge(s_cnt, 1)
            nc.vector.memset(RES[:, 0, :], 0.0).then_inc(s_res, 1)
            nc.vector.memset(emv[:, :], 0.0).then_inc(s_emv, 1)
            reg = [dve.value_load(cnti[0:1, 1, h:h + 1], min_val=0, max_val=SLOTS) for h in range(NE + 1)]

            def slot_norm(t):
                dve.wait_ge(s_ers, t + G + 1)
                dve.wait_ge(s_out, t * 16 + 16)
                ts(OUTN[:, :], RES[:, 0, :], emv[:, 0:1], emv[:, 3:4], ALU.subtract, ALU.mult).then_inc(s_outn, 1)

            for h in range(NE):
                with dve.Fori(reg[h], reg[h + 1]) as t:
                    for k in range(2):
                        dve.wait_ge(s_h, t * 4 + k + 3)
                        for c in (2 * k, 2 * k + 1):
                            last = ts(HE[:, NF + c, :], ps[:, 2 + k, (c % 2) * P:(c % 2 + 1) * P], EB1[:, (h + 1) % NE, c:c + 1], 0.0, ALU.add, ALU.max)
                        last.then_inc(s_hb, 1)
                    slot_norm(t)
                    dve.wait_ge(s_ye, t + 1)
                    dve.wait_ge(s_xb, t + 1)
                    dve.wait_ge(s_outn, t + 1)
                    stt(out=RES[:, 0, :], in0=ps[:, 4, 0:P], scalar=0.5, in1=XBS[:, :], op0=ALU.mult, op1=ALU.add).then_inc(s_res, 1)
                    dve.wait_ge(s_res, t + 2)
                    nc.vector.bn_stats(est[:, :], RES[:, 0, :]).then_inc(s_est, 1)
                    dve.wait_ge(s_cnt, 1)
                    dve.wait_ge(s_est, t + 1)
                    nc.vector.bn_aggr(emv[:, 0:2], est[:, :]).then_inc(s_emv, 1)
            slot_norm(reg[NE])

        @block.gpsimd
        def _(pool):
            ts, tt = nc.gpsimd.tensor_scalar, nc.gpsimd.tensor_tensor
            nc.gpsimd.memset(VA[:, :], 1.0).then_inc(s_va1, 1)
            nc.gpsimd.memset(fill[:, 0:P], 0.0).then_inc(s_fillm, 1)
            nc.gpsimd.memset(fill[:, P:ROW], NO_TOKEN).then_inc(s_fillm, 1)
            pool.wait_ge(s_fillm, 2)
            pool.dma_start(sorted_scr.rearrange("(s p) r -> p s r", p=P),
                           fill[:, None, :].to_broadcast([P, SLOTS, ROW])).then_inc(s_out, 16)
            for g in range(G):
                pool.wait_ge(s_add, g + 1)
                tt(X[:, cs(g)], X[:, cs(g)], ADD[:, cs(g)], ALU.add).then_inc(s_2x, 1)

            def low(t, g, src, rest):
                pool.wait_ge(s_hi[t], g + 1)
                tt(rest[:, cs(g)], src[:, cs(g)], PART[:, g % 2, 0, :], ALU.subtract).then_inc(s_r1[t], 1)
                pool.wait_ge(s_mid[t], g + 1)
                tt(PART[:, g % 2, 2, :], rest[:, cs(g)], PART[:, g % 2, 1, :], ALU.subtract).then_inc(s_lo[t], 1)

            for g in range(G):
                pool.wait_ge(s_n8[0], g + 1)
                ts(V[:, cs(g)], V[:, cs(g)], KNW, KNB, ALU.mult, ALU.add).then_inc(s_aff[0], 1)
                low(0, g, V, QP)
            for g in range(G):
                pool.wait_ge(s_norm[2], g + 1)
                tt(rows_of(X, g), rows_of(N, g), rows[:, 2, :][:, None, :].to_broadcast([P, GB, P]), ALU.add).then_inc(s_x1b, 1)
            for g in range(G):
                pool.wait_ge(s_n8[1], g + 1)
                ts(V[:, cs(g)], V[:, cs(g)], QNW, QNB, ALU.mult, ALU.add).then_inc(s_aff[1], 1)
                pool.wait_ge(s_aff[1], g + 1)
                tt(rows_of(ADD, g), rows_of(V, g), K["cos"][:, None, :].to_broadcast([P, GB, P]), ALU.mult).then_inc(s_t1, 1)
            for g in range(G):
                low(1, g, ADD, KP)
            pool.wait_ge(s_att, G)
            pool.wait_ge(s_num, G)
            nc.gpsimd.tensor_copy(X2[:, :, P:ROW], token_no[:, :, None].to_broadcast([P, B, ROW - P])).then_inc(s_x2id, 1)
            pool.wait_ge(ld_eb2, 16)
            pool.wait_ge(s_qc, G)
            tt(EB2P[:, 0:NE - 1, :], EB2[:, 0:NE - 1, :], EB2[:, 1:NE, :], ALU.add)
            tt(EB2P[:, NE - 1, :], EB2[:, NE - 1, :], EB2[:, 0, :], ALU.add).then_inc(s_eb2, 1)
            pool.wait_ge(s_eb2, 1)
            ts(EB2P[:, :, :], EB2P[:, :, :], 0.5, 1.0, ALU.mult, ALU.mult).then_inc(s_eb2, 1)
            pool.wait_ge(s_pos, 1)
            pool.wait_ge(s_x2, G)
            pool.wait_ge(s_out, 16)
            for b in range(B):
                pool.indirect_dma_start(sorted_scr, bass.IndirectOffsetOnAxis(ap=posu[:, b:b + 1], axis=0),
                                        X2[:, b, :], None).then_inc(s_sort, 16)
            pool.wait_ge(s_sc, 4 * B)
            nc.gpsimd.memset(XS[:, 0, P:ROW], NO_TOKEN).then_inc(s_eb2, 1)
            pool.wait_ge(s_xs, 16)
            pool.wait_ge(s_cnt, 1)
            pool.wait_ge(s_eb2, 3)
            last_row = pool.to_reg(NTOK - 1)
            reg = [pool.value_load(cnti[0:1, 1, h:h + 1], min_val=0, max_val=SLOTS) for h in range(NE + 1)]

            def slot_out(t):
                pool.wait_ge(s_out, t * 16 + 16)
                nc.gpsimd.tensor_copy(tok_u[:, :], XS[:, bass.ds(t, 1), P:P + 1].rearrange("p a e -> p (a e)")).then_inc(s_tok, 1)
                pool.wait_ge(s_cnt, 1)
                pool.wait_ge(s_tok, t + 1)
                pool.wait_ge(s_outn, t + 1)
                pool.indirect_dma_start(out_rows, bass.IndirectOffsetOnAxis(ap=tok_u[:, 0:1], axis=0),
                                        OUTN[:, :], None, bounds_check=last_row, oob_is_err=False).then_inc(s_out, 16)

            for h in range(NE):
                with pool.Fori(reg[h], reg[h + 1]) as t:
                    pool.wait_ge(s_res, t + 1)
                    tt(XBS[:, :], XS[:, bass.ds(t + 1, 1), 0:P].rearrange("p a e -> p (a e)"), EB2P[:, h, :], ALU.add).then_inc(s_xb, 1)
                    slot_out(t)
            pool.wait_ge(s_res, reg[NE] + 1)
            slot_out(reg[NE])
            pool.wait_ge(s_cnt, 1)
            pool.wait_ge(s_out, reg[NE] * 16 + 32)


def kernel(**inputs):
    import numpy as _np
    import concourse.bacc as _bacc
    from concourse import mybir as _mybir
    from concourse.bass_utils import run_bass_kernel_spmd as _run

    nc = _bacc.Bacc("TRN2", target_bir_lowering=False, num_devices=1)
    arrays, args = {}, []
    a = {n: _np.ascontiguousarray(v) for n, v in inputs.items()}

    def give(name, v):
        arrays[name] = v = _np.ascontiguousarray(v)
        args.append(nc.dram_tensor(name, v.shape, _mybir.dt.from_np(v.dtype), kind="ExternalInput").ap())

    def per_unit(v):
        return _np.moveaxis(v.reshape(v.shape[:-1] + (NF, P)), -1, 0)

    def per_head(v):
        return _np.tile(_np.repeat(v, 8), 2)

    give("in_x_dram", a["x"])
    give("in_ctx_dram", a["ctx_1024"])
    give("in_attn_w_dram", _np.stack([a["L0_attn_wq"].reshape(P, P), a["L0_attn_wk"].reshape(P, P),
                                      a["L0_attn_wv"].reshape(P, P), a["L0_attn_wo"].reshape(P, P)]))
    give("in_w1_dram", a["L0_attn_w1"])
    give("in_w2_dram", a["L0_attn_w2"])
    kv_b = a["L0_xattn_kv_b"]
    give("in_col_params_dram", _np.stack(
        [a["L0_attn_gamma1"], a["L0_attn_beta1"], a["L0_xattn_q_b"], kv_b[:P]]
        + [per_head(a[f"L0_xattn_{n}"]) for n in ("qn_w", "qn_b", "kn_w", "kn_b")]
        + list(a["L0_attn_b1"].reshape(NF, P)), 1))
    give("in_row_params_dram", _np.stack([a["L0_attn_b2"], kv_b[P:], a["L0_xattn_out_b"]]))
    kv_w = a["L0_xattn_kv_w"]
    place = _np.arange(H)
    head = 8 * (place % 4 // 2) + 2 * (place // 4) + place % 2
    out_w = a["L0_xattn_out_w"].reshape(P, H, HD)[:, head].reshape(P, P)
    give("in_xw_dram", _np.stack([a["L0_xattn_q_w"], kv_w[:P], kv_w[P:], out_w]))
    give("in_eW1_dram", a["L0_ffn_W1"])
    give("in_eb1_dram", per_unit(a["L0_ffn_b1"]))
    give("in_eW2_dram", a["L0_ffn_W2"])
    give("in_eb2_dram", a["L0_ffn_b2"])
    give("in_constants_dram", constants())
    give("in_ones_dram", _np.ones((1, H // 2, NTOK), _mybir.dt.np(BF16)))
    args.append(nc.dram_tensor("out_0_dram", (B, P, P), F32, kind="ExternalOutput").ap())
    decoder_layer(nc, *args)
    r = _run(nc, [arrays], core_ids=[0])
    return r.results[0]["out_0_dram"]
```
